# Optimizing a Trainium2 kernel written in Bass

```python
import numpy as np
import jax
import jax.numpy as jnp

def _softmax(x, axis=-1):
    return jax.nn.softmax(x, axis=axis)

def _gelu(x):
    return jax.nn.gelu(x, approximate=True)

def _silu(x):
    return jax.nn.silu(x)

def _sigmoid(x):
    return jax.nn.sigmoid(x)

def _layernorm(x, axis=-1, eps=1e-05):
    m = jnp.mean(x, axis=axis, keepdims=True)
    v = jnp.var(x, axis=axis, keepdims=True)
    return (x - m) / jnp.sqrt(v + eps)

def _scatter_add(tgt, idx, src, axis=0):
    return tgt.at[idx].add(src)

def _segment_sum(src, seg, n):
    return jax.ops.segment_sum(src, seg, n)
kernel_name = 'mk_flamingo_gated_d2_seqx_r4_a4b20e'

def setup_inputs(seed: int=0):
    np.random.seed(seed)
    _w = jnp.asarray

    def _rec_inputs():
        import jax
        import jax.numpy as jnp
        _rk = jax.random.key(seed)
        x = -0.0002928 + 1 * jax.random.normal(jax.random.fold_in(_rk, 1), (16, 256, 256), jnp.float32)
        _lenS = 256 - jax.random.randint(jax.random.fold_in(_rk, 7), (16,), 0, max(1, 256 // 4) + 1, jnp.int32)
        _lenS2 = 256 - jax.random.randint(jax.random.fold_in(_rk, 8), (16,), 0, max(1, 256 // 4) + 1, jnp.int32)
        _ctx_1024P = jax.random.normal(jax.random.fold_in(_rk, 11), (16, 16, 256), jnp.float32)
        _ctx_1024c = jax.random.dirichlet(jax.random.fold_in(_rk, 511), 0.3 * jnp.ones((16,), jnp.float32), (16, 256))
        _ctx_1024t = jnp.einsum('bsk,bkd->bsd', _ctx_1024c, _ctx_1024P)
        _ctx_1024t = _ctx_1024t * jax.lax.rsqrt(jnp.mean(jnp.square(_ctx_1024t)) + 1e-12) * 0.953939
        ctx_1024 = -1.39393e-06 + 0.999914 * (_ctx_1024t + 0.3 * jax.random.normal(jax.random.fold_in(_rk, 611), (16, 256, 256), jnp.float32))
        itok_BxSx2_0_63 = jax.random.randint(jax.random.fold_in(_rk, 12), (16, 256, 2), 0, 64, jnp.int32)
        _validS = jnp.arange(256)[None, :] < _lenS[:, None]
        _validS2 = jnp.arange(256)[None, :] < _lenS2[:, None]
        _causal = jnp.tril(jnp.ones((256, 256), dtype=bool))
        mask_Bx1xSxS2_ik1 = jnp.where(jnp.broadcast_to(_validS2[:, None, None, :], (16, 1, 256, 256)), 1, 0).astype(jnp.int32)
        _g = jax.random.normal(jax.random.fold_in(_rk, 9001), (2, 2), jnp.float32)
        _g = jnp.sign(_g) * jnp.maximum(jnp.abs(_g), 1.0) + (_g == 0) * 1.0
        g_xattn = _g[0]
        g_ffn = _g[1]
        return (x, ctx_1024, itok_BxSx2_0_63, mask_Bx1xSxS2_ik1, g_xattn, g_ffn)
    x, ctx_1024, itok_BxSx2_0_63, mask_Bx1xSxS2_ik1, g_xattn, g_ffn = _rec_inputs()

    def _L0_xattn_setup():
        import jax, jax.numpy as jnp
        import numpy as np
        ROPE_BASE = 100.0

        def _rope1d(tok, pos1d, base=ROPE_BASE):
            d = tok.shape[-1]
            inv_freq = 1.0 / base ** (jnp.arange(0, d, 2, dtype=jnp.float32) / d)
            ang = pos1d.astype(jnp.float32)[..., None] * inv_freq
            ang = jnp.concatenate([ang, ang], axis=-1)
            cos = jnp.cos(ang)[:, None]
            sin = jnp.sin(ang)[:, None]
            x1, x2 = jnp.split(tok, 2, axis=-1)
            rot = jnp.concatenate([-x2, x1], axis=-1)
            return tok * cos + rot * sin

        def _rope2d(tok, pos):
            ty, tx = jnp.split(tok, 2, axis=-1)
            ty = _rope1d(ty, pos[..., 0])
            tx = _rope1d(tx, pos[..., 1])
            return jnp.concatenate([ty, tx], axis=-1)
        key = jax.random.key(seed)
        ks = jax.random.split(key, 16)
        B, Nq, Nk, dim, H = (2, 512, 512, 256, 16)
        s = dim ** (-0.5)
        inp = {'query': jax.random.normal(ks[0], (B, Nq, dim), jnp.float32), 'key': jax.random.normal(ks[1], (B, Nk, dim), jnp.float32), 'value': jax.random.normal(ks[2], (B, Nk, dim), jnp.float32), 'Wq': jax.random.normal(ks[3], (dim, dim), jnp.float32) * s, 'bq': jnp.zeros((dim,), jnp.float32), 'Wk': jax.random.normal(ks[4], (dim, dim), jnp.float32) * s, 'bk': jnp.zeros((dim,), jnp.float32), 'Wv': jax.random.normal(ks[5], (dim, dim), jnp.float32) * s, 'bv': jnp.zeros((dim,), jnp.float32), 'Wp': jax.random.normal(ks[6], (dim, dim), jnp.float32) * s, 'bp': jnp.zeros((dim,), jnp.float32), 'qpos': jax.random.randint(ks[7], (B, Nq, 2), 0, 64, jnp.int64 if jax.config.jax_enable_x64 else jnp.int32), 'kpos': jax.random.randint(ks[8], (B, Nk, 2), 0, 64, jnp.int64 if jax.config.jax_enable_x64 else jnp.int32), 'num_cls': 1}
        return inp
    _L0_xattn_all = _L0_xattn_setup()
    _L0_xattn_in = {k: v for k, v in _L0_xattn_all.items() if k in ('Wq', 'bq', 'Wk', 'bk', 'Wv', 'bv', 'Wp', 'bp')}
    del _L0_xattn_all

    def _L0_ffn_setup():
        import jax, jax.numpy as jnp
        import numpy as np
        DIM = 256
        INTER = 512
        E = 8
        TOPK = 2
        ROUTE_SCALE = 1.0

        def _mlp(x, w1, w2, w3):
            h = jax.nn.silu(x @ w1.T) * (x @ w3.T)
            return h @ w2.T
        key = jax.random.key(seed)
        ks = jax.random.split(key, 10)
        s_in = 0.02
        return {'x': jax.random.normal(ks[0], (4, 512, DIM), dtype=jnp.float32), 'gate_w': jax.random.normal(ks[1], (E, DIM), dtype=jnp.float32) * s_in, 'gate_bias': jax.random.normal(ks[2], (E,), dtype=jnp.float32) * 0.01, 'w1': jax.random.normal(ks[3], (E, INTER, DIM), dtype=jnp.float32) * s_in, 'w2': jax.random.normal(ks[4], (E, DIM, INTER), dtype=jnp.float32) * s_in, 'w3': jax.random.normal(ks[5], (E, INTER, DIM), dtype=jnp.float32) * s_in, 'sw1': jax.random.normal(ks[6], (INTER, DIM), dtype=jnp.float32) * s_in, 'sw2': jax.random.normal(ks[7], (DIM, INTER), dtype=jnp.float32) * s_in, 'sw3': jax.random.normal(ks[8], (INTER, DIM), dtype=jnp.float32) * s_in}
    _L0_ffn_all = _L0_ffn_setup()
    _L0_ffn_in = {k: v for k, v in _L0_ffn_all.items() if k in ('gate_w', 'gate_bias', 'w1', 'w2', 'w3', 'sw1', 'sw2', 'sw3')}
    del _L0_ffn_all

    def _L1_xattn_setup():
        import jax, jax.numpy as jnp
        import numpy as np
        D_MODEL = 256
        NUM_HEADS = 16
        DIM_HEAD = 64
        B, NQ, NKV = (2, 512, 512)
        key = jax.random.key(seed)
        ks = jax.random.split(key, 12)
        inner = NUM_HEADS * DIM_HEAD
        s_in = 1.0 / np.sqrt(D_MODEL)
        s_o = 1.0 / np.sqrt(inner)
        return {'Q': jax.random.normal(ks[0], (B, NQ, D_MODEL), jnp.float32), 'K': jax.random.normal(ks[1], (B, NKV, D_MODEL), jnp.float32), 'V': jax.random.normal(ks[2], (B, NKV, D_MODEL), jnp.float32), 'mask': jax.random.randint(ks[3], (B, 1, NQ, NKV), 0, 2, jnp.int32), 'W_q': jax.random.normal(ks[4], (D_MODEL, inner), jnp.float32) * s_in, 'b_q': jnp.zeros((inner,), jnp.float32), 'W_k': jax.random.normal(ks[5], (D_MODEL, inner), jnp.float32) * s_in, 'b_k': jnp.zeros((inner,), jnp.float32), 'W_v': jax.random.normal(ks[6], (D_MODEL, inner), jnp.float32) * s_in, 'b_v': jnp.zeros((inner,), jnp.float32), 'W_o': jax.random.normal(ks[7], (inner, D_MODEL), jnp.float32) * s_o, 'b_o': jnp.zeros((D_MODEL,), jnp.float32)}
    _L1_xattn_all = _L1_xattn_setup()
    _L1_xattn_in = {k: v for k, v in _L1_xattn_all.items() if k in ('W_q', 'b_q', 'W_k', 'b_k', 'W_v', 'b_v', 'W_o', 'b_o')}
    del _L1_xattn_all

    def _L1_ffn_setup():
        import jax, jax.numpy as jnp
        import numpy as np
        QMAX = 127.0

        def _ste_round(v):
            return v + jax.lax.stop_gradient(jnp.round(v) - v)

        def _act_fake_quant(x, clip_factor):
            scale = jax.nn.sigmoid(clip_factor) * jnp.max(jnp.abs(x)) / QMAX
            return jnp.clip(_ste_round(x / scale), -QMAX - 1.0, QMAX) * scale

        def _weight_fake_quant(w):
            scale = jnp.max(jnp.abs(w), axis=1, keepdims=True) / QMAX
            return jnp.clip(_ste_round(w / scale), -QMAX - 1.0, QMAX) * scale
        key = jax.random.key(seed)
        k1, k2, k3, k4 = jax.random.split(key, 4)
        B, S, H, I = (8, 2048, 256, 704)
        return {'x': jax.random.normal(k1, (B, S, H), dtype=jnp.float32), 'clip_x': jnp.full((1,), 4.0, dtype=jnp.float32), 'clip_down': jnp.full((1,), 4.0, dtype=jnp.float32), 'w_gate': jax.random.normal(k2, (I, H), dtype=jnp.float32) * 0.02, 'w_up': jax.random.normal(k3, (I, H), dtype=jnp.float32) * 0.02, 'w_down': jax.random.normal(k4, (H, I), dtype=jnp.float32) * 0.02}
    _L1_ffn_all = _L1_ffn_setup()
    _L1_ffn_in = {k: v for k, v in _L1_ffn_all.items() if k in ('clip_x', 'clip_down', 'w_gate', 'w_up', 'w_down')}
    del _L1_ffn_all
    return {'x': x, 'ctx_1024': ctx_1024, 'itok_BxSx2_0_63': itok_BxSx2_0_63, 'mask_Bx1xSxS2_ik1': mask_Bx1xSxS2_ik1, 'g_xattn': g_xattn, 'g_ffn': g_ffn, 'L0_xattn_Wq': _L0_xattn_in['Wq'], 'L0_xattn_bq': _L0_xattn_in['bq'], 'L0_xattn_Wk': _L0_xattn_in['Wk'], 'L0_xattn_bk': _L0_xattn_in['bk'], 'L0_xattn_Wv': _L0_xattn_in['Wv'], 'L0_xattn_bv': _L0_xattn_in['bv'], 'L0_xattn_Wp': _L0_xattn_in['Wp'], 'L0_xattn_bp': _L0_xattn_in['bp'], 'L0_ffn_gate_w': _L0_ffn_in['gate_w'], 'L0_ffn_gate_bias': _L0_ffn_in['gate_bias'], 'L0_ffn_w1': _L0_ffn_in['w1'], 'L0_ffn_w2': _L0_ffn_in['w2'], 'L0_ffn_w3': _L0_ffn_in['w3'], 'L0_ffn_sw1': _L0_ffn_in['sw1'], 'L0_ffn_sw2': _L0_ffn_in['sw2'], 'L0_ffn_sw3': _L0_ffn_in['sw3'], 'L1_xattn_W_q': _L1_xattn_in['W_q'], 'L1_xattn_b_q': _L1_xattn_in['b_q'], 'L1_xattn_W_k': _L1_xattn_in['W_k'], 'L1_xattn_b_k': _L1_xattn_in['b_k'], 'L1_xattn_W_v': _L1_xattn_in['W_v'], 'L1_xattn_b_v': _L1_xattn_in['b_v'], 'L1_xattn_W_o': _L1_xattn_in['W_o'], 'L1_xattn_b_o': _L1_xattn_in['b_o'], 'L1_ffn_clip_x': _L1_ffn_in['clip_x'], 'L1_ffn_clip_down': _L1_ffn_in['clip_down'], 'L1_ffn_w_gate': _L1_ffn_in['w_gate'], 'L1_ffn_w_up': _L1_ffn_in['w_up'], 'L1_ffn_w_down': _L1_ffn_in['w_down']}

def reference(x, ctx_1024, itok_BxSx2_0_63, mask_Bx1xSxS2_ik1, g_xattn, g_ffn, L0_xattn_Wq, L0_xattn_bq, L0_xattn_Wk, L0_xattn_bk, L0_xattn_Wv, L0_xattn_bv, L0_xattn_Wp, L0_xattn_bp, L0_ffn_gate_w, L0_ffn_gate_bias, L0_ffn_w1, L0_ffn_w2, L0_ffn_w3, L0_ffn_sw1, L0_ffn_sw2, L0_ffn_sw3, L1_xattn_W_q, L1_xattn_b_q, L1_xattn_W_k, L1_xattn_b_k, L1_xattn_W_v, L1_xattn_b_v, L1_xattn_W_o, L1_xattn_b_o, L1_ffn_clip_x, L1_ffn_clip_down, L1_ffn_w_gate, L1_ffn_w_up, L1_ffn_w_down):
    import jax
    import jax.numpy as jnp

    def _L0_xattn_ref(query, key, value, Wq, bq, Wk, bk, Wv, bv, Wp, bp, qpos, kpos, num_cls):
        import jax, jax.numpy as jnp
        import numpy as np
        ROPE_BASE = 100.0

        def _rope1d(tok, pos1d, base=ROPE_BASE):
            d = tok.shape[-1]
            inv_freq = 1.0 / base ** (jnp.arange(0, d, 2, dtype=jnp.float32) / d)
            ang = pos1d.astype(jnp.float32)[..., None] * inv_freq
            ang = jnp.concatenate([ang, ang], axis=-1)
            cos = jnp.cos(ang)[:, None]
            sin = jnp.sin(ang)[:, None]
            x1, x2 = jnp.split(tok, 2, axis=-1)
            rot = jnp.concatenate([-x2, x1], axis=-1)
            return tok * cos + rot * sin

        def _rope2d(tok, pos):
            ty, tx = jnp.split(tok, 2, axis=-1)
            ty = _rope1d(ty, pos[..., 0])
            tx = _rope1d(tx, pos[..., 1])
            return jnp.concatenate([ty, tx], axis=-1)
        B, Nq, C = query.shape
        Nk = key.shape[1]
        H = 16
        Dh = C // H
        scale = Dh ** (-0.5)
        nc = int(num_cls)

        def split_heads(x, W, b, N):
            return (x @ W.T + b).reshape(B, N, H, Dh).transpose(0, 2, 1, 3)
        q = split_heads(query, Wq, bq, Nq)
        k = split_heads(key, Wk, bk, Nk)
        v = split_heads(value, Wv, bv, Nk)
        q_nc = _rope2d(q[:, :, nc:], qpos[:, nc:])
        k_nc = _rope2d(k[:, :, nc:], kpos[:, nc:])
        sim_rope = jnp.einsum('bhqd,bhkd->bhqk', q_nc, k_nc)
        if nc > 0:
            sim_qcls_k = jnp.einsum('bhqd,bhkd->bhqk', q[:, :, :nc], k[:, :, nc:])
            sim_q = jnp.einsum('bhqd,bhkd->bhqk', q, k[:, :, :nc])
            sim = jnp.concatenate([sim_qcls_k, sim_rope], axis=-2)
            sim = jnp.concatenate([sim_q, sim], axis=-1)
        else:
            sim = sim_rope
        attn = jax.nn.softmax(sim * scale, axis=-1)
        x = jnp.einsum('bhqk,bhkd->bhqd', attn, v)
        x = x.transpose(0, 2, 1, 3).reshape(B, Nq, C)
        return x @ Wp.T + bp

    def _L0_ffn_ref(x, gate_w, gate_bias, w1, w2, w3, sw1, sw2, sw3):
        import jax, jax.numpy as jnp
        import numpy as np
        DIM = 256
        INTER = 512
        E = 8
        TOPK = 2
        ROUTE_SCALE = 1.0

        def _mlp(x, w1, w2, w3):
            h = jax.nn.silu(x @ w1.T) * (x @ w3.T)
            return h @ w2.T
        shape = x.shape
        xt = x.reshape(-1, DIM)
        T = xt.shape[0]
        logits = xt @ gate_w.T
        scores = jax.nn.softmax(logits.astype(jnp.float32), axis=-1)
        original_scores = scores
        biased = scores + gate_bias
        _, indices = jax.lax.top_k(biased, TOPK)
        weights = jnp.take_along_axis(original_scores, indices, axis=1)
        weights = (weights * ROUTE_SCALE).astype(x.dtype)
        combine = (jax.nn.one_hot(indices, E, dtype=weights.dtype) * weights[..., None]).sum(axis=1)
        y = jnp.zeros_like(xt)
        for e in range(E):
            y = y + _mlp(xt, w1[e], w2[e], w3[e]) * combine[:, e:e + 1]
        z = _mlp(xt, sw1, sw2, sw3)
        return (y + z).reshape(shape)

    def _L1_xattn_ref(Q, K, V, mask, W_q, b_q, W_k, b_k, W_v, b_v, W_o, b_o):
        import jax, jax.numpy as jnp
        import numpy as np
        D_MODEL = 256
        NUM_HEADS = 16
        DIM_HEAD = 64
        B, NQ, NKV = (2, 512, 512)
        h, d = (NUM_HEADS, DIM_HEAD)

        def split_heads(x):
            b, n, _ = x.shape
            return x.reshape(b, n, h, d).transpose(0, 2, 1, 3)
        q = split_heads(Q @ W_q + b_q)
        k = split_heads(K @ W_k + b_k)
        v = split_heads(V @ W_v + b_v)
        scores = jnp.einsum('bhqd,bhkd->bhqk', q, k) / jnp.sqrt(jnp.float32(d))
        scores = jnp.where(mask == 0, jnp.float32(-1000000000.0), scores)
        probs = jax.nn.softmax(scores, axis=-1)
        out = jnp.einsum('bhqk,bhkd->bhqd', probs, v)
        out = out.transpose(0, 2, 1, 3).reshape(Q.shape[0], Q.shape[1], h * d)
        return out @ W_o + b_o

    def _L1_ffn_ref(x, clip_x, clip_down, w_gate, w_up, w_down):
        import jax, jax.numpy as jnp
        import numpy as np
        QMAX = 127.0

        def _ste_round(v):
            return v + jax.lax.stop_gradient(jnp.round(v) - v)

        def _act_fake_quant(x, clip_factor):
            scale = jax.nn.sigmoid(clip_factor) * jnp.max(jnp.abs(x)) / QMAX
            return jnp.clip(_ste_round(x / scale), -QMAX - 1.0, QMAX) * scale

        def _weight_fake_quant(w):
            scale = jnp.max(jnp.abs(w), axis=1, keepdims=True) / QMAX
            return jnp.clip(_ste_round(w / scale), -QMAX - 1.0, QMAX) * scale
        xq = _act_fake_quant(x, clip_x[0])
        gate = jnp.einsum('bsh,ih->bsi', xq, _weight_fake_quant(w_gate))
        up = jnp.einsum('bsh,ih->bsi', xq, _weight_fake_quant(w_up))
        h = _act_fake_quant(jax.nn.silu(gate) * up, clip_down[0])
        return jnp.einsum('bsi,hi->bsh', h, _weight_fake_quant(w_down))
    x = x + jnp.tanh(g_xattn[0]) * _L0_xattn_ref(_layernorm(x, axis=-1), ctx_1024, ctx_1024, L0_xattn_Wq, L0_xattn_bq, L0_xattn_Wk, L0_xattn_bk, L0_xattn_Wv, L0_xattn_bv, L0_xattn_Wp, L0_xattn_bp, itok_BxSx2_0_63, itok_BxSx2_0_63, 1)
    x = x + jnp.tanh(g_ffn[0]) * _L0_ffn_ref(_layernorm(x, axis=-1), L0_ffn_gate_w, L0_ffn_gate_bias, L0_ffn_w1, L0_ffn_w2, L0_ffn_w3, L0_ffn_sw1, L0_ffn_sw2, L0_ffn_sw3)
    x = x + jnp.tanh(g_xattn[1]) * _L1_xattn_ref(_layernorm(x, axis=-1), ctx_1024, ctx_1024, mask_Bx1xSxS2_ik1, L1_xattn_W_q, L1_xattn_b_q, L1_xattn_W_k, L1_xattn_b_k, L1_xattn_W_v, L1_xattn_b_v, L1_xattn_W_o, L1_xattn_b_o)
    x = x + jnp.tanh(g_ffn[1]) * _L1_ffn_ref(_layernorm(x, axis=-1), L1_ffn_clip_x, L1_ffn_clip_down, L1_ffn_w_gate, L1_ffn_w_up, L1_ffn_w_down)
    return x

_drawn_inputs = setup_inputs


def setup_inputs(seed=0):
    import zlib

    import numpy as np

    out = dict(_drawn_inputs(seed))
    spreads = {'g_ffn': (-1.0, 0.6),
     'L0_xattn_bq': (0.0, 0.722),
     'L0_xattn_bk': (0.0, 0.8),
     'L0_xattn_bv': (0.0, 0.1),
     'L0_xattn_bp': (0.0, 0.1),
     'L1_xattn_b_q': (0.0, 2.0),
     'L1_xattn_b_k': (0.0, 2.0),
     'L1_xattn_b_v': (0.0, 0.66),
     'L1_xattn_b_o': (0.0, 0.685)}
    factors = {'L0_ffn_gate_w': 8.0,
     'L0_ffn_gate_bias': 8.0,
     'L0_ffn_w1': 8.0,
     'L0_ffn_w2': 8.0,
     'L0_ffn_w3': 8.0,
     'L0_ffn_sw1': 3.703,
     'L0_ffn_sw2': 3.667,
     'L0_ffn_sw3': 3.658,
     'L1_ffn_w_gate': 2.852,
     'L1_ffn_w_up': 2.736,
     'L1_ffn_w_down': 2.711}
    for name, (base, spread) in spreads.items():
        noise = np.random.default_rng([zlib.crc32(name.encode()), seed]).standard_normal(out[name].shape)
        drawn = base * np.exp(spread * noise) if base else spread * noise
        out[name] = jnp.asarray(drawn.astype(out[name].dtype))
    for name, factor in factors.items():
        out[name] = (out[name] * factor).astype(out[name].dtype)
    return out
```

```python
import concourse.bass as bass
from concourse import mybir
from contextlib import ExitStack
import math
import numpy as np

F32 = mybir.dt.float32
F16 = mybir.dt.float16
BF16 = mybir.dt.bfloat16
I32 = mybir.dt.int32
U32 = mybir.dt.uint32
ACT = mybir.ActivationFunctionType
ALU = mybir.AluOpType
AX = mybir.AxisListType

B, S, D = 16, 256, 256
P = 128
TILES = B * S // P
KD = D // P
H = 16
EPS = 1e-5
ROUND = 1.5 * 2.0 ** 23


class Counter:

    def __init__(self, sem, per, start=1):
        self.sem, self.per, self.start = sem, per, start

    def wait(self, eng, b, k):
        eng.wait_ge(self.sem, b * self.per + k + self.start)


class Chain:

    def __init__(self, sem, per):
        self.sem, self.per = sem, per

    def begin(self, b):
        self.b, self.k = b, 0

    def link(self, eng, ins):
        self.k += 1
        ins.then_inc(self.sem, 1)
        eng.wait_ge(self.sem, self.b * self.per + self.k)

    def end(self):
        assert self.k == self.per, (self.k, self.per)


class Scope:

    taken = []

    def __init__(self, nc, ctx, tag):
        self.nc, self.ctx, self.tag = nc, ctx, tag

    def sb(self, name, shape, dt=F32):
        return self.ctx.enter_context(self.nc.sbuf_tensor(f"{self.tag}_{name}", shape, dt))

    def ps(self, name, shape, dt=F32):
        return self.ctx.enter_context(self.nc.psum_tensor(f"{self.tag}_{name}", shape, dt))

    def sem(self, name):
        sem = self.nc.alloc_semaphore(f"{self.tag}_{name}")
        Scope.taken.append(sem)
        return sem

    def counter(self, name, per, start=1):
        sig = Counter(self.sem(name), per, start)
        if start:
            self.nc.sync.sem_inc(sig.sem, start)
        return sig

    def chain(self, name, per):
        return Chain(self.sem(name), per)


def end_of_part(nc):
    nc.clear_and_free_semaphores(list(Scope.taken))
    Scope.taken.clear()
    nc.all_engine_barrier()


def three_products(nc, out, a_hi, a_lo, b_hi, b_lo, chunks):
    n = 0
    last = None
    for kt in range(chunks):
        for a, b in ((a_hi, b_hi), (a_hi, b_lo), (a_lo, b_hi)):
            last = nc.tensor.matmul(out, a(kt), b(kt), start=(n == 0), stop=(n == 3 * chunks - 1))
            n += 1
    return last


def setup_phase(nc, ctx, X, x_d, itok_d, g_x_d, g_f_d, consts):
    ident, ident16, identb, is0, not0, cosT, sinT, gates = consts
    s = Scope(nc, ctx, "su")
    pos_i = s.sb("pos_i", [P, TILES, 2], I32)
    pos = s.sb("pos", [P, TILES, 2])
    ang = s.sb("ang", [P, TILES, 2, 4])
    turns = s.sb("turns", [P, TILES, 2, 4])
    red = s.sb("red", [P, TILES, 2, 4])
    mag = s.sb("mag", [P, TILES, 2, 4])
    sn = s.sb("sn", [P, TILES, 2, 4])
    cs = s.sb("cs", [P, TILES, 2, 4])
    graw = s.sb("graw", [P, 4])
    x_in, pos_in, g_in = s.sem("x_in"), s.sem("pos_in"), s.sem("g_in")
    pool_steps, masks_ready, reduced = s.sem("pool_steps"), s.sem("masks_ready"), s.sem("reduced")
    sin_ready, dve_steps = s.sem("sin_ready"), s.sem("dve_steps")
    inv = (1.0 / (np.float32(100.0) ** (np.arange(0, 8, 2, dtype=np.float32) / np.float32(8)))).astype(np.float32)
    two_pi_hi = 6.28125
    two_pi_mid = float(np.float32(2 * math.pi - two_pi_hi))
    two_pi_lo = 2 * math.pi - two_pi_hi - two_pi_mid
    with nc.Block() as block:
        @block.sync
        def _(sp):
            sp.dma_start(pos_i[:], itok_d.rearrange("(t p) c -> p t c", p=P)).then_inc(pos_in, 16)
            sp.dma_start(graw[:, 0:2], g_x_d.partition_broadcast(P)).then_inc(g_in, 16)
            sp.dma_start(graw[:, 2:4], g_f_d.partition_broadcast(P)).then_inc(g_in, 16)
            sp.dma_start(X[:], x_d.rearrange("(t p) d -> p t d", p=P)).then_inc(x_in, 16)
            sp.wait_ge(x_in, 16)

        @block.gpsimd
        def _(pool):
            n = 0
            for m in (ident, ident16, identb):
                nc.gpsimd.memset(m[:], 0.0).then_inc(pool_steps, 1)
                n += 1
                pool.wait_ge(pool_steps, n)
                nc.gpsimd.affine_select(out=m[:], in_=m[:], compare_op=ALU.not_equal, fill=1.0, base=0,
                                        pattern=[[-1, P]], channel_multiplier=1).then_inc(pool_steps, 1)
                n += 1
            nc.gpsimd.memset(is0[:], 0.0).then_inc(pool_steps, 1)
            nc.gpsimd.memset(not0[:], 1.0).then_inc(pool_steps, 1)
            n += 2
            pool.wait_ge(pool_steps, n)
            nc.gpsimd.affine_select(out=is0[:], in_=is0[:], compare_op=ALU.not_equal, fill=1.0, base=0,
                                    pattern=[[0, 1]], channel_multiplier=1).then_inc(masks_ready, 1)
            nc.gpsimd.affine_select(out=not0[:], in_=not0[:], compare_op=ALU.not_equal, fill=0.0, base=0,
                                    pattern=[[0, 1]], channel_multiplier=1).then_inc(masks_ready, 1)

        @block.vector
        def _(dve):
            ch = Chain(dve_steps, 0)
            ch.begin(0)

            def link(ins):
                ch.link(dve, ins)

            dve.wait_ge(pos_in, 16)
            link(nc.vector.tensor_copy(pos[:], pos_i[:]))
            for j in range(4):
                link(nc.vector.tensor_scalar(ang[:, :, :, j], pos[:], float(inv[j]), None, ALU.mult))
            link(nc.vector.tensor_scalar(turns[:], ang[:], 1.0 / (2 * math.pi), ROUND, ALU.mult, ALU.add))
            link(nc.vector.tensor_scalar(turns[:], turns[:], ROUND, None, ALU.subtract))
            f = "p t c j -> p (t c j)"
            r2, t2, a2 = red[:].rearrange(f), turns[:].rearrange(f), ang[:].rearrange(f)
            link(nc.vector.scalar_tensor_tensor(r2, t2, -two_pi_hi, a2, ALU.mult, ALU.add))
            link(nc.vector.scalar_tensor_tensor(r2, t2, -two_pi_mid, r2, ALU.mult, ALU.add))
            link(nc.vector.scalar_tensor_tensor(r2, t2, -two_pi_lo, r2, ALU.mult, ALU.add))
            link(nc.vector.tensor_scalar(red[:], red[:], 3.1415925, -3.1415925, ALU.min, ALU.max))
            link(nc.vector.tensor_scalar(mag[:], red[:], -1.0, None, ALU.mult))
            link(nc.vector.tensor_tensor(mag[:], mag[:], red[:], ALU.max))
            nc.vector.tensor_scalar(mag[:], mag[:], -1.0, math.pi / 2, ALU.mult, ALU.add).then_inc(reduced, 1)
            dve.wait_ge(sin_ready, 2)
            dve.wait_ge(masks_ready, 2)
            se = sn[:].rearrange("p (b e) c j -> p b e (c j)", e=2)[:, :, 0, :]
            ce = cs[:].rearrange("p (b e) c j -> p b e (c j)", e=2)[:, :, 0, :]
            link(nc.vector.tensor_scalar(se, se, not0[:, 0:1], None, ALU.mult))
            link(nc.vector.tensor_scalar(ce, ce, not0[:, 0:1], None, ALU.mult))
            cv = cosT[:].rearrange("p t (c i j) -> p t c i j", c=2, i=2)
            sv = sinT[:].rearrange("p t (c i j) -> p t c i j", c=2, i=2)
            for i in range(2):
                link(nc.vector.tensor_copy(cv[:, :, :, i, :], cs[:]))
                link(nc.vector.tensor_scalar(sv[:, :, :, i, :], sn[:], 2.0 * i - 1.0, None, ALU.mult))

        @block.scalar
        def _(act):
            act.wait_ge(g_in, 32)
            nc.scalar.activation(gates[:], graw[:], ACT.Tanh)
            act.wait_ge(reduced, 1)
            nc.scalar.activation(sn[:], red[:], ACT.Sin).then_inc(sin_ready, 1)
            nc.scalar.activation(cs[:], mag[:], ACT.Sin).then_inc(sin_ready, 1)


def tile_stats(nc, X, st, t):
    return nc.vector.bn_stats(st[:, bass.ds(t, 1), :].rearrange("p a s -> p (a s)"), X[:, bass.ds(t, 1), :].rearrange("p a d -> p (a d)"))


def layernorm_stats(nc, ctx, tag, X, st, mean, rstd, whole=False):
    s = Scope(nc, ctx, tag)
    dm = s.sb("dm", [P, TILES])
    v = s.sb("v", [P, TILES])
    t = s.sb("t", [P, TILES])
    r = s.sb("r", [P, TILES])
    stats_done, steps, var_ready, root_ready = s.sem("stats_done"), s.sem("steps"), s.sem("var_ready"), s.sem("root_ready")
    with nc.Block() as block:
        @block.vector
        def _(dve):
            if whole:
                with dve.Fori(0, TILES // 4) as i:
                    for u in range(4):
                        last = tile_stats(nc, X, st, i * 4 + u)
                    last.then_inc(stats_done, 1)
                dve.wait_ge(stats_done, TILES // 4)
            ch = Chain(steps, 0)
            ch.begin(0)

            def link(ins):
                ch.link(dve, ins)

            link(nc.vector.tensor_tensor(dm[:], st[:, :, 1], st[:, :, 4], ALU.subtract))
            link(nc.vector.tensor_tensor(mean[:], st[:, :, 1], st[:, :, 4], ALU.add))
            link(nc.vector.tensor_scalar(mean[:], mean[:], 0.5, None, ALU.mult))
            link(nc.vector.tensor_tensor(dm[:], dm[:], dm[:], ALU.mult))
            link(nc.vector.tensor_tensor(v[:], st[:, :, 2], st[:, :, 5], ALU.add))
            link(nc.vector.tensor_scalar(v[:], v[:], 1.0 / D, EPS, ALU.mult, ALU.add))
            link(nc.vector.scalar_tensor_tensor(v[:], dm[:], 0.25, v[:], ALU.mult, ALU.add))
            dve.sem_inc(var_ready, 1)
            dve.wait_ge(root_ready, 1)
            link(nc.vector.reciprocal(r[:], t[:]))
            link(nc.vector.tensor_tensor(dm[:], r[:], r[:], ALU.mult))
            link(nc.vector.tensor_tensor(dm[:], dm[:], v[:], ALU.mult))
            link(nc.vector.tensor_scalar(dm[:], dm[:], -0.5, 1.5, ALU.mult, ALU.add))
            link(nc.vector.tensor_tensor(rstd[:], r[:], dm[:], ALU.mult))

        @block.scalar
        def _(act):
            act.wait_ge(var_ready, 1)
            nc.scalar.activation(t[:], v[:], ACT.Sqrt).then_inc(root_ready, 1)


def load_split(nc, ctx, tag, jobs, width, beside=None):
    s = Scope(nc, ctx, tag)
    NS = min(len(jobs), 4)
    stage = [s.sb(f"stage{i}", [P, width]) for i in range(NS)]
    loaded = [s.sem(f"loaded{i}") for i in range(NS)]
    hi_ready, lo_ready = s.sem("hi_ready"), s.sem("lo_ready")
    with nc.Block() as block:
        @block.sync
        def _(sp):
            for n, (src, hi, lo) in enumerate(jobs):
                if n >= NS:
                    sp.wait_ge(lo_ready, n - NS + 1)
                sp.dma_start(stage[n % NS][:, 0:width].rearrange("p (a b) -> p a b", a=src.shape[1]), src)\
                    .then_inc(loaded[n % NS], 16)

        @block.scalar
        def _(act):
            for n, (src, hi, lo) in enumerate(jobs):
                act.wait_ge(loaded[n % NS], 16 * (n // NS + 1))
                nc.scalar.activation(hi, stage[n % NS][:], ACT.Copy).then_inc(hi_ready, 1)

        @block.vector
        def _(dve):
            for n, (src, hi, lo) in enumerate(jobs):
                dve.wait_ge(hi_ready, n + 1)
                nc.vector.tensor_tensor(lo, stage[n % NS][:], hi, ALU.subtract).then_inc(lo_ready, 1)
                if beside:
                    beside[1](dve, n, len(jobs))

        if beside:
            @block.gpsimd
            def _(pool):
                beside[0](pool)


def none():
    pass


def spread(turns, *plans):
    def turn(n):
        for plan in plans:
            for do in plan.get(n, []):
                do()
    return [lambda n=n: turn(n) for n in range(turns)]


def pipeline(eng, front, back):
    def run(steps_front, steps_back):
        for k in range(max(len(steps_front), len(steps_back))):
            if k < len(steps_front):
                steps_front[k]()
            if k < len(steps_back):
                steps_back[k]()

    run(front(0, 0), [])
    with eng.Fori(0, B // 2 - 1) as i:
        b = i * 2
        run(front(b + 1, 1), back(b, 0))
        run(front(b + 2, 0), back(b + 1, 1))
    run(front(B - 1, 1), back(B - 2, 0))
    run([], back(B - 1, 1))


def attention0(nc, ctx, X, mean, rstd, ctxT_d, w_d, bias_d, consts):
    ident, ident16, identb, is0, not0, cosT, sinT, gates = consts
    s = Scope(nc, ctx, "a0")
    dh = D // H
    W = {n: (s.sb(f"w{n}h", [P, KD * D], F16), s.sb(f"w{n}l", [P, KD * D], F16)) for n in "qkvp"}
    bias = s.sb("bias", [P, 4, D])
    with ExitStack() as c2:
        load_split(nc, c2, "w0", [(w_d[n].rearrange("(k p) n -> p k n", p=P), W[n][0][:], W[n][1][:]) for n in "qkvp"], KD * D)
    Wv = {n: tuple(t[:].rearrange("p (k n) -> p k n", k=KD) for t in W[n]) for n in "qkvp"}

    GW = 64
    MROW = 32
    PAIRS = H // 2
    ctxin = s.sb("ctxin", [P, KD, S])
    ch, cl = s.sb("ch", [P, KD, S], F16), s.sb("cl", [P, KD, S], F16)
    xn = s.sb("xn", [P, 2, D])
    xh, xl = s.sb("xh", [P, KD, S], F16), s.sb("xl", [P, KD, S], F16)
    raw = s.sb("raw", [P, 2, D])
    rc = s.sb("rc", [P, 2, D])
    rs = s.sb("rs", [P, 2, D])
    Qst, Kst = s.sb("Qst", [P, 2, H, GW]), s.sb("Kst", [P, 2, H, GW])
    Qst16 = s.sb("Qst16", [P, 2, H, GW], F16)
    Vst = [s.sb(f"Vst{i}", [P, 2, H, 32]) for i in range(2)]
    K32 = [[s.sb(f"K32_{i}{h}", [P, PAIRS, S]) for h in range(2)] for i in range(2)]
    Q32 = [s.sb(f"Q32_{i}", [P, PAIRS, S]) for i in range(2)]
    K16 = s.sb("K16", [P, PAIRS, S], F16)
    Q16 = [s.sb(f"Q16_{h}", [P, PAIRS, S], F16) for h in range(2)]
    M = s.sb("M", [P, 2, H])
    PT = [s.sb(f"PT{i}", [P, 2, S]) for i in range(8)]
    OT = s.sb("OT", [P, 4, S])
    rec = s.sb("rec", [P, 2, H])
    O = s.sb("O", [P, 2, D])
    oh, ol = s.sb("oh", [P, KD, S], F16), s.sb("ol", [P, KD, S], F16)
    proj = s.sb("proj", [P, 2, D])

    pF = [s.ps(f"pF{i}", [P, 512]) for i in range(2)]
    pS = [s.ps(f"pS{i}", [P, 2, S]) for i in range(2)]
    flat = [t[:].rearrange("p h t -> p (h t)") for t in pS]
    K_BANKS, Q16_BANKS, Q32_BANKS = (*flat, pF[0][:], pF[1][:]), flat, (pF[0][:], pF[1][:], *flat)
    pT = [s.ps(f"pT{i}", [P, 2, S]) for i in range(2)]
    pO = s.ps("pO", [P, S])
    pG = s.ps("pG", [P, 512])

    consts_in, cleared, keys_cleared = s.sem("consts_in"), s.sem("cleared"), s.sem("keys_cleared")
    ctx_in, ctx_hi, ctx_lo = s.counter("ctx_in", 16), s.counter("ctx_hi", 1), s.counter("ctx_lo", 1)
    xn_ready, x_hi, x_lo = s.counter("xn_ready", 1), s.counter("x_hi", 1), s.counter("x_lo", 1)
    f_full = s.counter("f_full", 14)
    k_raw, q_raw, v_ready = s.counter("k_raw", 1), s.counter("q_raw", 1), s.counter("v_ready", 1)
    stack_ready = s.counter("stack_ready", 3)
    k32_ready, k16_ready = s.counter("k32_ready", 4), s.counter("k16_ready", 4)
    q16_ready, q32_ready = s.counter("q16_ready", 2), s.counter("q32_ready", 4)
    s_full, s_max = s.counter("s_full", 16), s.counter("s_max", 16)
    t_full, p_ready = s.counter("t_full", 16), s.counter("p_ready", 16)
    pv_full, pv_out = s.counter("pv_full", 4), s.counter("pv_out", 4)
    g_full = s.counter("g_full", 4)
    o_ready, o_hi, o_lo, x_done = s.counter("o_ready", 2), s.counter("o_hi", 1), s.counter("o_lo", 1), s.counter("x_done", 1)
    front_steps, back_steps = s.chain("front_steps", 3), s.chain("back_steps", 3)

    FRONT, SC, LAST = (0, 1, 2, 4), (5, 6, 7, 8, 10, 10, 11, 12), 13
    ST, PV, END = (0, 1, 2, 4, 4, 5, 7, 9), (2, 5, 6, 10), (11, 12, 13)
    TURNS, AHEAD = 14, 7

    def front_order(steps, scores, last, ahead=[]):
        return spread(TURNS, *[{t: [do]} for t, do in zip(FRONT, steps)],
                      *([{t: [scores(2 * k, 2 * k + 2)]} for k, t in enumerate(SC)] if scores else []), {LAST: [last]}, {AHEAD: ahead})

    def back_order(st, pv, lag, end):
        return spread(TURNS, *([{t: [lambda p2=p2: st(p2)]} for p2, t in enumerate(ST)] if st else []),
                      *([{t + lag: [lambda g=g: pv(g)]} for g, t in enumerate(PV)] if pv else []), *[{t: [do]} for t, do in zip(END, end)])

    with nc.Block() as block:
        @block.sync
        def _(sp):
            for i, n in enumerate("qkvp"):
                sp.dma_start(bias[:, i, :], bias_d[n].partition_broadcast(P)).then_inc(consts_in, 16)
            src = ctxT_d.rearrange("(k p) t -> p k t", p=P)
            with sp.Fori(0, B) as b:
                ctx_lo.wait(sp, b, 0)
                sp.dma_start(ctxin[:], src[:, :, bass.ts(b, S)]).then_inc(ctx_in.sem, 16)

        @block.gpsimd
        def _(pool):
            zeroed = [Qst, Kst, Qst16, *Vst, Q16[0], Q16[1]]
            for t in zeroed:
                nc.gpsimd.memset(t[:], 0.0).then_inc(cleared, 1)
            pool.wait_ge(cleared, len(zeroed))
            for t in Vst:
                nc.gpsimd.memset(t[:, :, :, dh:dh + 1], 1.0).then_inc(cleared, 1)
            nc.gpsimd.memset(Kst[:, :, :, MROW:MROW + 1], 1.0).then_inc(cleared, 1)

            with pool.Fori(0, B) as b:
                ctx_hi.wait(pool, b, 1)
                nc.gpsimd.tensor_tensor(cl[:], ctxin[:], ch[:], ALU.subtract).then_inc(ctx_lo.sem, 1)

        CLEARED = 10

        @block.tensor
        def _(pe):
            pe.wait_ge(cleared, CLEARED)
            pe.wait_ge(keys_cleared, 4)

            def transpose_pairs(b, job, bank, stack, pairs, idn):
                for a, p2 in enumerate(pairs):
                    for j in range(2):
                        last = nc.tensor.transpose(bank[:, a * S + j * P:a * S + (j + 1) * P],
                                                   stack[:, j, 2 * p2:2 * p2 + 2, :].rearrange("p h r -> p (h r)"), idn[:])
                last.then_inc(f_full.sem, 1)

            def front(b, par):
                def project(job, n, ah, al):
                    for j in range(2):
                        last = three_products(nc, pF[job % 2][:, j * D:(j + 1) * D],
                                              lambda kt: ah[:, kt, j * P:(j + 1) * P], lambda kt: al[:, kt, j * P:(j + 1) * P],
                                              lambda kt: Wv[n][0][:, kt, :], lambda kt: Wv[n][1][:, kt, :], KD)
                    last.then_inc(f_full.sem, 1)

                def inputs():
                    xn_ready.wait(pe, b, 1)
                    q32_ready.wait(pe, b, 0)
                    for kt in range(KD):
                        for j in range(2):
                            last = nc.tensor.transpose(pF[0][:, kt * S + j * P:kt * S + (j + 1) * P],
                                                       xn[:, j, kt * P:(kt + 1) * P], ident[:])
                    last.then_inc(f_full.sem, 1)
                    ctx_lo.wait(pe, b, 1)
                    project(1, "k", ch, cl)

                def inputs_rest():
                    x_lo.wait(pe, b, 1)
                    project(2, "v", ch, cl)
                    k_raw.wait(pe, b, 1)
                    project(3, "q", xh, xl)

                def k_transposes():
                    stack_ready.wait(pe, b, 1)
                    for q in range(4):
                        if q >= 2:
                            (v_ready, q_raw)[q - 2].wait(pe, b, 1)
                        transpose_pairs(b, 4 + q, K_BANKS[q], Kst, (2 * q, 2 * q + 1), ident)

                def q_transposes():
                    stack_ready.wait(pe, b, 2)
                    for q in range(2):
                        k16_ready.wait(pe, b, 1 + q)
                        transpose_pairs(b, 8 + q, Q16_BANKS[q].bitcast(F16), Qst16, range(4 * q, 4 * q + 4), ident16)

                def scores(k0, k1):
                    def go():
                        if k0 == 0:
                            k16_ready.wait(pe, b, 4)
                            q16_ready.wait(pe, b, 2)
                        for k in range(k0, k1):
                            p2, j = k // 2, k % 2
                            s_max.wait(pe, b, max(k - 1, 0))
                            for h in range(2):
                                last = nc.tensor.matmul(pS[k % 2][:, h, :], Q16[h][:, p2, j * P:(j + 1) * P], K16[:, p2, :],
                                                        start=True, stop=True)
                            last.then_inc(s_full.sem, 1)
                    return go

                def q32_transposes():
                    stack_ready.wait(pe, b, 3)
                    for q in range(4):
                        if q < 2:
                            k16_ready.wait(pe, b, 3 + q)
                        transpose_pairs(b, 10 + q, Q32_BANKS[q], Qst, (2 * q, 2 * q + 1), ident)
                return front_order([inputs, inputs_rest, k_transposes, q_transposes], scores, q32_transposes)

            def back(b, par):
                def st(p2):
                    if p2 == 0:
                        k32_ready.wait(pe, b, 4)
                        q32_ready.wait(pe, b, 4)
                    for h in (2 * p2, 2 * p2 + 1):
                        p_ready.wait(pe, b, max(h - 1, 0))
                        for kt in range(2):
                            last = nc.tensor.matmul(pT[h % 2][:, kt, :], K32[par][h % 2][:, h // 2, kt * P:(kt + 1) * P],
                                                    Q32[par][:, h // 2, :], start=True, stop=True)
                        last.then_inc(t_full.sem, 1)

                def pv(g):
                    if g == 0:
                        v_ready.wait(pe, b, 1)
                    p_ready.wait(pe, b, 4 * g + 4)
                    pv_out.wait(pe, b, g)
                    for kt in range(2):
                        for a in range(4):
                            h = 4 * g + a
                            last = nc.tensor.matmul(pO[32 * a:32 * a + 32, :], Vst[par][:, kt, h, :], PT[h % 8][:, kt, :],
                                                    start=(kt == 0), stop=(kt == 1))
                    last.then_inc(pv_full.sem, 1)

                def by_token():
                    pv_out.wait(pe, b, 4)
                    for j in range(2):
                        (x_done, o_ready)[j].wait(pe, b, j)
                        for g in range(4):
                            last = nc.tensor.transpose(pG[:, g * P:(g + 1) * P], OT[:, g, j * P:(j + 1) * P], ident[:])
                        last.then_inc(g_full.sem, 1)

                def by_width():
                    o_ready.wait(pe, b, 2)
                    for kt in range(KD):
                        for j in range(2):
                            last = nc.tensor.transpose(pG[:, kt * S + j * P:kt * S + (j + 1) * P],
                                                       O[:, j, kt * P:(kt + 1) * P], ident[:])
                    last.then_inc(g_full.sem, 1)

                def output():
                    o_lo.wait(pe, b, 1)
                    for j in range(2):
                        last = three_products(nc, pG[:, j * D:(j + 1) * D],
                                              lambda kt: oh[:, kt, j * P:(j + 1) * P], lambda kt: ol[:, kt, j * P:(j + 1) * P],
                                              lambda kt: Wv["p"][0][:, kt, :], lambda kt: Wv["p"][1][:, kt, :], KD)
                    last.then_inc(g_full.sem, 1)
                return back_order(st, pv, 0, [by_token, by_width, output])

            pipeline(pe, front, back)

        @block.scalar
        def _(act):
            act.wait_ge(cleared, CLEARED)
            act.wait_ge(keys_cleared, 4)

            def context_high(b, first):
                if not first:
                    f_full.wait(act, b, 3 - f_full.per)
                ctx_in.wait(act, b, 16)
                nc.scalar.activation(ch[:], ctxin[:], ACT.Copy).then_inc(ctx_hi.sem, 1)

            def ahead(b):
                return [lambda: context_high(b + 1, False)] if not isinstance(b, int) or b < B - 1 else []

            def front(b, par):
                def inputs():
                    f_full.wait(act, b, 1)
                    nc.scalar.activation(xh[:].rearrange("p k t -> p (k t)"), pF[0][:], ACT.Copy).then_inc(x_hi.sem, 1)

                def k_copies():
                    for q in range(4):
                        f_full.wait(act, b, 5 + q)
                        for h in range(2):
                            last = nc.scalar.activation(K32[par][h][64 * h:64 * h + 64, 2 * q:2 * q + 2, :].rearrange("p a t -> p (a t)"),
                                                        K_BANKS[q][64 * h:64 * h + 64, :], ACT.Copy)
                        last.then_inc(k32_ready.sem, 1)

                def q32_copies():
                    for q in range(4):
                        f_full.wait(act, b, 11 + q)
                        nc.scalar.activation(Q32[par][:, 2 * q:2 * q + 2, :].rearrange("p a t -> p (a t)"), Q32_BANKS[q],
                                             ACT.Copy).then_inc(q32_ready.sem, 1)
                return front_order([inputs, none, k_copies], None, q32_copies, ahead(b))

            def back(b, par):
                def exps(p2):
                    pv_full.wait(act, b, max(p2 // 2 - 1, 0))
                    for h in (2 * p2, 2 * p2 + 1):
                        t_full.wait(act, b, h + 1)
                        nc.scalar.activation(PT[h % 8][:], pT[h % 2][:], ACT.Exp, scale=float(dh) ** -0.5).then_inc(p_ready.sem, 1)

                def finish():
                    g_full.wait(act, b, 3)
                    nc.scalar.activation(oh[:].rearrange("p k t -> p (k t)"), pG[:], ACT.Copy).then_inc(o_hi.sem, 1)
                return back_order(exps, None, 0, [none, finish, none])

            context_high(0, True)
            pipeline(act, front, back)

        @block.vector
        def _(dve):
            for t in [t for par in K32 for t in par]:
                nc.vector.memset(t[:], 0.0).then_inc(keys_cleared, 1)
            dve.wait_ge(cleared, CLEARED)
            dve.wait_ge(consts_in, 64)

            def heads(ap):
                return ap.rearrange("p (h d) -> p h d", h=H)

            def normalised(b, first):
                if not first:
                    f_full.wait(dve, b, 1 - f_full.per)
                for j in range(2):
                    t = 2 * b + j
                    last = nc.vector.tensor_scalar(xn[:, j, :], X[:, bass.ds(t, 1), :].rearrange("p a d -> p (a d)"),
                                                   mean[:, bass.ds(t, 1)], rstd[:, bass.ds(t, 1)], ALU.subtract, ALU.mult)
                last.then_inc(xn_ready.sem, 1)

            def ahead(b):
                return [lambda: normalised(b + 1, False)] if not isinstance(b, int) or b < B - 1 else []

            def front(b, par):
                def link(ins):
                    front_steps.link(dve, ins)

                def rope(stack):
                    for j in range(2):
                        t = 2 * b + j
                        cb = cosT[:, bass.ds(t, 1), :].broadcast_to([P, H, dh])
                        nc.vector.tensor_tensor(heads(rc[:, j, :]), heads(raw[:, j, :]), cb, ALU.mult)
                        for i in range(2):
                            swapped = heads(raw[:, j, :]).rearrange("p h (c i j) -> p h c i j", c=2, i=2)[:, :, :, 1 - i, :]
                            out = heads(rs[:, j, :]).rearrange("p h (c i j) -> p h c i j", c=2, i=2)[:, :, :, i, :]
                            sb = sinT[:, bass.ds(t, 1), :].rearrange("p a (c i j) -> p a c i j", c=2, i=2)[:, :, :, i, :].broadcast_to([P, H, 2, 4])
                            ins = nc.vector.tensor_tensor(out, swapped, sb, ALU.mult)
                    link(ins)
                    return nc.vector.tensor_tensor(stack[:, :, :, 0:dh].rearrange("p t h d -> p (t h) d"),
                                                   rc[:].rearrange("p t (h d) -> p (t h) d", h=H),
                                                   rs[:].rearrange("p t (h d) -> p (t h) d", h=H), ALU.add)

                def inputs():
                    front_steps.begin(b)
                    x_hi.wait(dve, b, 1)
                    nc.vector.tensor_tensor(xl[:].rearrange("p k t -> p (k t)"), pF[0][:], xh[:].rearrange("p k t -> p (k t)"),
                                            ALU.subtract).then_inc(x_lo.sem, 1)
                    f_full.wait(dve, b, 2)
                    nc.vector.tensor_tensor(raw[:], pF[1][:].rearrange("p (t d) -> p t d", t=2),
                                            bias[:, 1:2, :].broadcast_to([P, 2, D]), ALU.add).then_inc(k_raw.sem, 1)
                    k_raw.wait(dve, b, 1)
                    rope(Kst)
                    nc.vector.tensor_scalar(Kst[:, 0, :, dh:2 * dh], heads(raw[:, 0, :]), is0[:, 0:1], None, ALU.mult)
                    nc.vector.tensor_scalar(Kst[:, 0, :, MROW + 1:MROW + 1 + dh], heads(raw[:, 0, :]), not0[:, 0:1], None, ALU.mult)
                    nc.vector.tensor_copy(Kst[:, 1, :, MROW + 1:MROW + 1 + dh], heads(raw[:, 1, :])).then_inc(stack_ready.sem, 1)

                def inputs_rest():
                    f_full.wait(dve, b, 3)
                    nc.vector.tensor_tensor(Vst[par][:, :, :, 0:dh], pF[0][:].rearrange("p (t h d) -> p t h d", t=2, h=H),
                                            bias[:, 2:3, :].rearrange("p a (h d) -> p a h d", h=H).broadcast_to([P, 2, H, dh]), ALU.add).then_inc(v_ready.sem, 1)
                    f_full.wait(dve, b, 4)
                    stack_ready.wait(dve, b, 1)
                    nc.vector.tensor_tensor(raw[:], pF[1][:].rearrange("p (t d) -> p t d", t=2),
                                            bias[:, 0:1, :].broadcast_to([P, 2, D]), ALU.add).then_inc(q_raw.sem, 1)
                    q_raw.wait(dve, b, 1)
                    ins = rope(Qst)
                    nc.vector.tensor_copy(Qst[:, :, :, dh:2 * dh].rearrange("p t h d -> p (t h) d"),
                                          raw[:].rearrange("p t (h d) -> p (t h) d", h=H))
                    link(nc.vector.tensor_scalar(Qst[:, 0, :, MROW + 1:MROW + 1 + dh], heads(raw[:, 0, :]), is0[:, 0:1], None, ALU.mult))
                    nc.vector.tensor_copy(Qst16[:, :, :, 0:MROW].rearrange("p t h d -> p (t h) d"),
                                          Qst[:, :, :, 0:MROW].rearrange("p t h d -> p (t h) d"))
                    nc.vector.tensor_copy(Qst16[:, 0, :, MROW + 1:MROW + 1 + dh],
                                          Qst[:, 0, :, MROW + 1:MROW + 1 + dh]).then_inc(stack_ready.sem, 1)
                    front_steps.end()

                def k16_copies():
                    for q in range(4):
                        k32_ready.wait(dve, b, q + 1)
                        nc.vector.tensor_copy(K16[:, 2 * q:2 * q + 2, :].rearrange("p a t -> p (a t)"), K_BANKS[q])\
                            .then_inc(k16_ready.sem, 1)

                def q16_copies():
                    for q in range(2):
                        f_full.wait(dve, b, 9 + q)
                        src = Q16_BANKS[q].bitcast(F16)
                        for h in range(2):
                            last = nc.vector.tensor_copy(Q16[h][64 * h:64 * h + 64, 4 * q:4 * q + 4, :].rearrange("p a t -> p (a t)"),
                                                         src[64 * h:64 * h + 64, :])
                        last.then_inc(q16_ready.sem, 1)

                def maxima(k0, k1):
                    def go():
                        for k in range(k0, k1):
                            s_full.wait(dve, b, k + 1)
                            nc.vector.reduce_max(M[:, k % 2, k - k % 2:k - k % 2 + 2], pS[k % 2][:], AX.X).then_inc(s_max.sem, 1)
                        if k1 == 16:
                            s_max.wait(dve, b, 16)
                            nc.vector.tensor_scalar(Qst[:, :, :, MROW], M[:], -1.0, None, ALU.mult).then_inc(stack_ready.sem, 1)
                    return go
                return front_order([inputs, inputs_rest, k16_copies, q16_copies], maxima, none, ahead(b))

            def back(b, par):
                def out(g):
                    if g == 0:
                        g_full.wait(dve, b, 0)
                    pv_full.wait(dve, b, g + 1)
                    nc.vector.tensor_copy(OT[:, g, :], pO[:]).then_inc(pv_out.sem, 1)

                def normalise():
                    back_steps.begin(b)
                    for j in range(2):
                        g_full.wait(dve, b, j + 1)
                        sums = pG[:].rearrange("p (h r) -> p h r", r=32)
                        back_steps.link(dve, nc.vector.reciprocal(rec[:, j, :], sums[:, :, dh]))
                        nc.vector.tensor_tensor(heads(O[:, j, :]), sums[:, :, 0:dh], rec[:, j:j + 1, :].rearrange("p a h -> p h a").broadcast_to([P, H, dh]),
                                                ALU.mult).then_inc(o_ready.sem, 1)

                def low():
                    o_hi.wait(dve, b, 1)
                    nc.vector.tensor_tensor(ol[:].rearrange("p k t -> p (k t)"), pG[:], oh[:].rearrange("p k t -> p (k t)"),
                                            ALU.subtract).then_inc(o_lo.sem, 1)

                def residual():
                    g_full.wait(dve, b, 4)
                    back_steps.link(dve, nc.vector.tensor_tensor(proj[:], pG[:].rearrange("p (t d) -> p t d", t=2),
                                                                 bias[:, 3:4, :].broadcast_to([P, 2, D]), ALU.add))
                    xb = X[:, bass.ds(2 * b, 2), :].rearrange("p t d -> p (t d)")
                    nc.vector.scalar_tensor_tensor(xb, proj[:].rearrange("p t d -> p (t d)"), gates[:, 0:1], xb, ALU.mult, ALU.add)\
                        .then_inc(x_done.sem, 1)
                    back_steps.end()
                return back_order(None, out, 0, [normalise, low, residual])
            normalised(0, True)
            pipeline(dve, front, back)
            x_done.wait(dve, B, 0)


def attention1(nc, ctx, X, mean, rstd, ctxT_d, mask_d, maskT_d, w_d, bias_d, consts, combine):
    ident, ident16, identb, is0, not0, cosT, sinT, gates = consts
    s = Scope(nc, ctx, "a1")
    dh = 64
    INNER = H * dh
    PAIRS = H // 2
    MASKED = -2.0 ** 40
    W = {n: (s.sb(f"w{n}h", [P, KD * INNER], F16), s.sb(f"w{n}l", [P, KD * INNER], F16)) for n in "qkvo"}
    KH = [[s.sb(f"KH{i}{h}", [P, PAIRS, S], F16) for h in range(2)] for i in range(2)]
    KL = [[s.sb(f"KL{i}{h}", [P, PAIRS, S], F16) for h in range(2)] for i in range(2)]
    with ExitStack() as c2:
        on_pool, add_share = moe_combine(nc, c2, X, *combine) if combine else (lambda pool: None, lambda dve, n, jobs: None)

        def on_dve(dve, n, jobs):
            for t in (KH[n // 2][n % 2], KL[n // 2][n % 2]):
                nc.vector.memset(t[:], 0.0)
            add_share(dve, n, jobs)
        beside = (on_pool, on_dve)
        load_split(nc, c2, "w1", [(w_d[n].rearrange("(k p) n -> p k n", p=P), W[n][0][:], W[n][1][:]) for n in "qkvo"], KD * INNER, beside)
    if combine:
        with ExitStack() as c2:
            layernorm_stats(nc, c2, "l2", X, combine[0], mean, rstd)
    Wv = {n: tuple(t[:].rearrange("p (k n) -> p k n", k=PAIRS if n == "o" else KD) for t in W[n]) for n in "qkvo"}

    bqk = s.sb("bqk", [P, 2, PAIRS])
    bv = s.sb("bv", [P, INNER])
    bo = s.sb("bo", [P, D])
    ctxin = s.sb("ctxin", [P, KD, S])
    ch, cl = s.sb("ch", [P, KD, S], F16), s.sb("cl", [P, KD, S], F16)
    xn = s.sb("xn", [P, 2, D])
    xh, xl = s.sb("xh", [P, KD, S], F16), s.sb("xl", [P, KD, S], F16)
    maskin = s.sb("maskin", [P, 2, 2, S], I32)
    maskq = s.sb("maskq", [P, 2, S], BF16)
    maskk = [s.sb(f"maskk{i}", [P, 2, S], BF16) for i in range(2)]
    QH = [s.sb(f"QH{i}", [P, PAIRS, S], F16) for i in range(2)]
    QL = [s.sb(f"QL{i}", [P, PAIRS, S], F16) for i in range(2)]
    v32 = [s.sb(f"v32{i}", [P, 512]) for i in range(2)]
    VH, VL = [s.sb(f"VH{i}", [P, 2, INNER], F16) for i in range(2)], [s.sb(f"VL{i}", [P, 2, INNER], F16) for i in range(2)]
    ones = s.sb("ones", [P, dh], F16)
    lift = s.sb("lift", [P, 1])
    M, nM, nR = s.sb("M", [P, 2, H]), s.sb("nM", [P, 2, H]), s.sb("nR", [P, 2, H])
    NM = s.sb("NM", [P, 2, P // H, H], BF16)
    MT = [s.sb(f"MT{i}", [P, S], BF16) for i in range(2)]
    pick = s.sb("pick", [P, H, P], BF16)
    P32 = [s.sb(f"P32{i}", [P, 2, S]) for i in range(2)]
    PH, PL = [s.sb(f"PH{i}", [P, 2, S], F16) for i in range(4)], [s.sb(f"PL{i}", [P, 2, S], F16) for i in range(4)]
    OS = [s.sb(f"OS{i}", [P, 2, S]) for i in range(2)]
    R = s.sb("R", [P, S])
    ON = s.sb("ON", [P, 2, S])
    oh, ol = s.sb("oh", [P, PAIRS, S], F16), s.sb("ol", [P, PAIRS, S], F16)
    proj = s.sb("proj", [P, 2, D])

    pF = [s.ps(f"pF{i}", [P, 512]) for i in range(2)]
    pS = [s.ps(f"pS{i}", [P, 2, S]) for i in range(2)]
    BANKS = (pF[0][:], pF[1][:], *(t[:].rearrange("p h t -> p (h t)") for t in pS))
    pT = [s.ps(f"pT{i}", [P, 2, S]) for i in range(2)]
    pO = s.ps("pO", [P, 2, S])
    pG = s.ps("pG", [P, 512])

    consts_in, cleared = s.sem("consts_in"), s.sem("cleared")
    ctx_in, mask_in = s.counter("ctx_in", 16), s.counter("mask_in", 32)
    ctx_hi, ctx_lo, masks = s.counter("ctx_hi", 1), s.counter("ctx_lo", 1), s.counter("masks", 2)
    xn_ready, x_hi, x_lo = s.counter("xn_ready", 1), s.counter("x_hi", 1), s.counter("x_lo", 1)
    f_full = s.counter("f_full", 13)
    n_full = s.counter("n_full", 1)
    k_hi, k_lo = s.counter("k_hi", 4), s.counter("k_lo", 4)
    q_hi, q_lo = s.counter("q_hi", 4), s.counter("q_lo", 4)
    v_ready, neg_parts, neg_ready = s.counter("v_ready", 4), s.counter("neg_parts", 1), s.counter("neg_ready", 1)
    s_full, s_max = s.counter("s_full", 16), s.counter("s_max", 16)
    t_full, p_ready, pl_ready = s.counter("t_full", 16), s.counter("p_ready", 16), s.counter("pl_ready", 16)
    vh_ready, vl_ready = s.counter("vh_ready", 4), s.counter("vl_ready", 4)
    pv_full, pv_out, on_ready = s.counter("pv_full", PAIRS), s.counter("pv_out", PAIRS), s.counter("on_ready", PAIRS)
    o_hi, o_lo = s.counter("o_hi", PAIRS), s.counter("o_lo", PAIRS)
    g_full, x_done = s.counter("g_full", 1), s.counter("x_done", 1)
    neg_steps, back_steps = s.chain("neg_steps", 4), s.chain("back_steps", PAIRS + 1)

    ST, PV = (1, 3, 4, 6, 8, 10, 12, 13), (3, 5, 6, 9, 11, 12, 13, 14)
    KEYS, VALUES, QUERIES, SCORES = (0, 1, 1, 3), (3, 4, 5, 6), (6, 7, 9, 9), (10, 11, 12, 13, 14, 15, 17, 17)

    def front_order(first, keys, values, queries, scores, last, more={}):
        def jobs(turns, job):
            return [{turns[q]: [lambda q=q: job(q)]} for q in range(4)] if job else []
        score_jobs = [{SCORES[k]: [scores(2 * k, 2 * k + 2)]} for k in range(8)] if scores else []
        return spread(18, {0: first}, *jobs(KEYS, keys), *jobs(VALUES, values), *jobs(QUERIES, queries), more, *score_jobs, {17: last})

    with nc.Block() as block:
        @block.sync
        def _(sp):
            sp.dma_start(bqk[:, 0, :], bias_d["q"]).then_inc(consts_in, 16)
            sp.dma_start(bqk[:, 1, :], bias_d["k"]).then_inc(consts_in, 16)
            sp.dma_start(bv[:], bias_d["v"].partition_broadcast(P)).then_inc(consts_in, 16)
            sp.dma_start(bo[:], bias_d["o"].partition_broadcast(P)).then_inc(consts_in, 16)
            src = ctxT_d.rearrange("(k p) t -> p k t", p=P)
            mq = mask_d.rearrange("(t p) k -> p t k", p=P)
            mk = maskT_d.rearrange("(t p) q -> p t q", p=P)
            with sp.Fori(0, B) as b:
                ctx_lo.wait(sp, b, 0)
                sp.dma_start(ctxin[:], src[:, :, bass.ts(b, S)]).then_inc(ctx_in.sem, 16)
                masks.wait(sp, b, 0)
                sp.dma_start(maskin[:, 0, :, :], mq[:, bass.ds(2 * b, 2), :]).then_inc(mask_in.sem, 16)
                sp.dma_start(maskin[:, 1, :, :], mk[:, bass.ds(2 * b, 2), :]).then_inc(mask_in.sem, 16)

        @block.gpsimd
        def _(pool):
            zeroed = [pick, NM]
            for t in zeroed:
                nc.gpsimd.memset(t[:], 0.0).then_inc(cleared, 1)
            nc.gpsimd.memset(ones[:], 1.0).then_inc(cleared, 1)
            nc.gpsimd.memset(lift[:], math.log(1024.0)).then_inc(cleared, 1)
            n = len(zeroed) + 2
            for a in range(3):
                pool.wait_ge(cleared, n + a)
                nc.gpsimd.affine_select(out=pick[:], in_=pick[:], compare_op=ALU.not_equal, fill=1.0, base=-H * a,
                                        pattern=[[-1, H], [0, P]], channel_multiplier=1).then_inc(cleared, 1)

            def context_low(b):
                ctx_hi.wait(pool, b, 1)
                nc.gpsimd.tensor_tensor(cl[:], ctxin[:], ch[:], ALU.subtract).then_inc(ctx_lo.sem, 1)

            def front(b, par):
                def values(n):
                    j, half = n // 2, n % 2
                    vh_ready.wait(pool, b, n + 1)
                    cs = slice(half * 512, half * 512 + 512)
                    nc.gpsimd.tensor_tensor(VL[par][:, j, cs], v32[n % 2][:], VH[par][:, j, cs], ALU.subtract).then_inc(vl_ready.sem, 1)

                ahead = [] if isinstance(b, int) and b == B - 1 else [lambda: context_low(b + 1)]
                return front_order([], None, values, None, None, [], {9: ahead})

            def back(b, par):
                def low(p2):
                    o_hi.wait(pool, b, p2 + 1)
                    nc.gpsimd.tensor_tensor(ol[:, p2, :], ON[:, p2 % 2, :], oh[:, p2, :], ALU.subtract).then_inc(o_lo.sem, 1)

                def probs(p2):
                    for h in (2 * p2, 2 * p2 + 1):
                        p_ready.wait(pool, b, h + 1)
                        nc.gpsimd.tensor_tensor(PL[h % 4][:], P32[h % 2][:], PH[h % 4][:], ALU.subtract).then_inc(pl_ready.sem, 1)
                return spread(18, {ST[p2]: [lambda p2=p2: probs(p2)] for p2 in range(PAIRS)},
                              {PV[p2] + 2: [lambda p2=p2: low(p2)] for p2 in range(PAIRS)})
            context_low(0)
            pipeline(pool, front, back)

        CLEARED = 7

        @block.tensor
        def _(pe):
            pe.wait_ge(cleared, CLEARED)

            def front(b, par):
                def project(job, p0, wt, ah, al):
                    for a in range(2):
                        last = three_products(nc, BANKS[job % 4][:, a * S:(a + 1) * S],
                                              lambda kt: wt[0][:, kt, (p0 + a) * P:(p0 + a + 1) * P],
                                              lambda kt: wt[1][:, kt, (p0 + a) * P:(p0 + a + 1) * P],
                                              lambda kt: ah[:, kt, :], lambda kt: al[:, kt, :], KD)
                    last.then_inc(f_full.sem, 1)

                def inputs():
                    xn_ready.wait(pe, b, 1)
                    q_lo.wait(pe, b, 0)
                    s_max.wait(pe, b, 0)
                    for kt in range(KD):
                        for j in range(2):
                            last = nc.tensor.transpose(pF[0][:, kt * S + j * P:kt * S + (j + 1) * P],
                                                       xn[:, j, kt * P:(kt + 1) * P], ident[:])
                    last.then_inc(f_full.sem, 1)

                def keys(q):
                    ctx_lo.wait(pe, b, 1)
                    if q == 3:
                        x_lo.wait(pe, b, 1)
                    project(1 + q, 2 * q, Wv["k"], ch, cl)

                def values(n):
                    j, half = n // 2, n % 2
                    k_lo.wait(pe, b, n + 1)
                    last = three_products(nc, BANKS[(5 + n) % 4],
                                          lambda kt: ch[:, kt, j * P:(j + 1) * P], lambda kt: cl[:, kt, j * P:(j + 1) * P],
                                          lambda kt: Wv["v"][0][:, kt, half * 512:half * 512 + 512],
                                          lambda kt: Wv["v"][1][:, kt, half * 512:half * 512 + 512], KD)
                    last.then_inc(f_full.sem, 1)

                def queries(q):
                    v_ready.wait(pe, b, q + 1)
                    project(9 + q, 2 * q, Wv["q"], xh, xl)

                def scores(k0, k1):
                    def go():
                        if k0 == 0:
                            masks.wait(pe, b, 2)
                            q_lo.wait(pe, b, 4)
                            k_hi.wait(pe, b, 4)
                        for k in range(k0, k1):
                            p2, j = k // 2, k % 2
                            s_max.wait(pe, b, max(k - 1, 0))
                            for h in range(2):
                                nc.tensor.matmul(pS[k % 2][:, h, :], QH[par][:, p2, j * P:(j + 1) * P], KH[par][h][:, p2, :],
                                                 start=True, stop=False)
                                last = nc.tensor.matmul(pS[k % 2][:, h, :], identb[:], maskq[:, j, :], start=False, stop=True)
                            last.then_inc(s_full.sem, 1)
                    return go

                return front_order([inputs], keys, values, queries, scores, [])

            def back(b, par):
                def negated():
                    neg_parts.wait(pe, b, 1)
                    x_done.wait(pe, b, 0)
                    for j in range(2):
                        last = nc.tensor.transpose(pG[:, 0:P].bitcast(BF16)[:, j * P:(j + 1) * P],
                                                   NM[:, j, :, :].rearrange("p a h -> p (a h)"), identb[:])
                    last.then_inc(n_full.sem, 1)

                def pv(p2):
                    if p2 == 0:
                        vl_ready.wait(pe, b, 4)
                    pl_ready.wait(pe, b, 2 * p2 + 2)
                    pv_out.wait(pe, b, p2)
                    for what, parts in enumerate((((VH[par], PH), (VH[par], PL), (VL[par], PH)), ((None, PH), (None, PL)))):
                        n = 0
                        for kt in range(2):
                            for v, p in parts:
                                n += 1
                                for a in range(2):
                                    h = 2 * p2 + a
                                    lhs = v[:, kt, h * dh:(h + 1) * dh] if v is not None else ones[:]
                                    last = nc.tensor.matmul(pO[64 * a:64 * a + 64, what, :], lhs, p[h % 4][:, kt, :],
                                                            start=(n == 1), stop=(n == 2 * len(parts)))
                    last.then_inc(pv_full.sem, 1)

                def project(p2):
                    o_lo.wait(pe, b, p2 + 1)
                    for j in range(2):
                        ts = slice(j * P, (j + 1) * P)
                        for n, (a, w) in enumerate(((oh, 0), (oh, 1), (ol, 0))):
                            last = nc.tensor.matmul(pG[:, j * D:(j + 1) * D], a[:, p2, ts], Wv["o"][w][:, p2, :],
                                                    start=(p2 == 0 and j == 0 and n == 0), stop=(p2 == PAIRS - 1 and j == 1 and n == 2))
                    if p2 == PAIRS - 1:
                        last.then_inc(g_full.sem, 1)

                def st_pair(p2):
                    for h in (2 * p2, 2 * p2 + 1):
                        if h == 0:
                            k_lo.wait(pe, b, 4)
                            q_lo.wait(pe, b, 4)
                            neg_ready.wait(pe, b, 1)
                        p_ready.wait(pe, b, max(h - 1, 0))
                        for kt in range(2):
                            out = pT[h % 2][:, kt, :]
                            ks = slice(kt * P, (kt + 1) * P)
                            nc.tensor.matmul(out, KH[par][h % 2][:, p2, ks], QH[par][:, p2, :], start=True, stop=False)
                            nc.tensor.matmul(out, KH[par][h % 2][:, p2, ks], QL[par][:, p2, :], start=False, stop=False)
                            nc.tensor.matmul(out, KL[par][h % 2][:, p2, ks], QH[par][:, p2, :], start=False, stop=False)
                            nc.tensor.matmul(out, identb[:], maskk[par][:, kt, :], start=False, stop=False)
                            last = nc.tensor.matmul(out, pick[:, h, :], MT[par][:], start=False, stop=True)
                        last.then_inc(t_full.sem, 1)

                return spread(18, {0: [negated]}, {ST[p2]: [lambda p2=p2: st_pair(p2)] for p2 in range(PAIRS)},
                              {PV[p2]: [lambda p2=p2: pv(p2)] for p2 in range(PAIRS)},
                              {PV[p2] + 3: [lambda p2=p2: project(p2)] for p2 in range(PAIRS)})

            pipeline(pe, front, back)

        @block.scalar
        def _(act):
            act.wait_ge(cleared, CLEARED)
            act.wait_ge(consts_in, 64)

            def context_high(b, first):
                if not first:
                    f_full.wait(act, b, 9 - f_full.per)
                ctx_in.wait(act, b, 16)
                nc.scalar.activation(ch[:], ctxin[:], ACT.Copy).then_inc(ctx_hi.sem, 1)

            def ahead(b):
                return [lambda: context_high(b + 1, False)] if not isinstance(b, int) or b < B - 1 else []

            def front(b, par):
                def inputs():
                    f_full.wait(act, b, 1)
                    nc.scalar.activation(xh[:].rearrange("p k t -> p (k t)"), pF[0][:], ACT.Copy).then_inc(x_hi.sem, 1)

                def keys(q):
                    f_full.wait(act, b, 2 + q)
                    for a in range(2):
                        p2 = 2 * q + a
                        for h in range(2):
                            r = slice(64 * h, 64 * h + 64)
                            last = nc.scalar.activation(KH[par][h][r, p2, :], BANKS[(1 + q) % 4][r, a * S:(a + 1) * S],
                                                        ACT.Identity, bias=bqk[r, 1, p2:p2 + 1])
                    last.then_inc(k_hi.sem, 1)

                def queries(q):
                    f_full.wait(act, b, 10 + q)
                    for a in range(2):
                        p2 = 2 * q + a
                        last = nc.scalar.activation(QH[par][:, p2, :], BANKS[(9 + q) % 4][:, a * S:(a + 1) * S],
                                                    ACT.Identity, bias=bqk[:, 0, p2:p2 + 1])
                    last.then_inc(q_hi.sem, 1)

                def values(n):
                    j, half = n // 2, n % 2
                    v_ready.wait(act, b, n + 1)
                    nc.scalar.activation(VH[par][:, j, half * 512:half * 512 + 512], v32[n % 2][:], ACT.Copy).then_inc(vh_ready.sem, 1)
                return front_order([inputs], keys, values, queries, None, [], {8: ahead(b)})

            def back(b, par):
                def exps(p2):
                    pv_full.wait(act, b, max(p2 - 1, 0))
                    for h in (2 * p2, 2 * p2 + 1):
                        t_full.wait(act, b, h + 1)
                        nc.scalar.activation(PH[h % 4][:], pT[h % 2][:], ACT.Exp, bias=lift[:], scale=float(dh) ** -0.5)
                        pl_ready.wait(act, b, max(h - 1, 0))
                        nc.scalar.activation(P32[h % 2][:], pT[h % 2][:], ACT.Exp, bias=lift[:], scale=float(dh) ** -0.5)\
                            .then_inc(p_ready.sem, 1)

                def evacuate(p2):
                    pv_full.wait(act, b, p2 + 1)
                    on_ready.wait(act, b, max(p2 - 1, 0))
                    nc.scalar.activation(OS[p2 % 2][:], pO[:], ACT.Copy).then_inc(pv_out.sem, 1)

                def high(p2):
                    on_ready.wait(act, b, p2 + 1)
                    if p2 == 0:
                        g_full.wait(act, b, 0)
                    nc.scalar.activation(oh[:, p2, :], ON[:, p2 % 2, :], ACT.Copy).then_inc(o_hi.sem, 1)
                return spread(18, {ST[p2]: [lambda p2=p2: exps(p2)] for p2 in range(PAIRS)},
                              {PV[p2]: [lambda p2=p2: evacuate(p2)] for p2 in range(PAIRS)},
                              {PV[p2] + 2: [lambda p2=p2: high(p2)] for p2 in range(PAIRS)})

            context_high(0, True)
            pipeline(act, front, back)

        @block.vector
        def _(dve):
            dve.wait_ge(cleared, CLEARED)
            dve.wait_ge(consts_in, 64)

            def normalised(b, first):
                if not first:
                    f_full.wait(dve, b, 1 - f_full.per)
                for j in range(2):
                    t = 2 * b + j
                    last = nc.vector.tensor_scalar(xn[:, j, :], X[:, bass.ds(t, 1), :].rearrange("p a d -> p (a d)"),
                                                   mean[:, bass.ds(t, 1)], rstd[:, bass.ds(t, 1)], ALU.subtract, ALU.mult)
                last.then_inc(xn_ready.sem, 1)

            def ahead(b):
                return [lambda: normalised(b + 1, False)] if not isinstance(b, int) or b < B - 1 else []

            def front(b, par):
                def inputs():
                    x_hi.wait(dve, b, 1)
                    nc.vector.tensor_tensor(xl[:].rearrange("p k t -> p (k t)"), pF[0][:], xh[:].rearrange("p k t -> p (k t)"),
                                            ALU.subtract).then_inc(x_lo.sem, 1)

                def make_masks():
                    mask_in.wait(dve, b, 32)
                    for i, m in enumerate((maskq, maskk[par])):
                        nc.vector.tensor_scalar(m[:], maskin[:, i, :, :], 0.0, MASKED, ALU.is_equal, ALU.mult).then_inc(masks.sem, 1)

                def keys(q):
                    k_hi.wait(dve, b, q + 1)
                    for a in range(2):
                        p2 = 2 * q + a
                        for h in range(2):
                            r = slice(64 * h, 64 * h + 64)
                            last = nc.vector.scalar_tensor_tensor(KL[par][h][r, p2, :], BANKS[(1 + q) % 4][r, a * S:(a + 1) * S],
                                                                  bqk[r, 1, p2:p2 + 1], KH[par][h][r, p2, :], ALU.add, ALU.subtract)
                    last.then_inc(k_lo.sem, 1)

                def values(n):
                    j, half = n // 2, n % 2
                    f_full.wait(dve, b, 6 + n)
                    cs = slice(half * 512, half * 512 + 512)
                    vl_ready.wait(dve, b, max(n - 1, 0))
                    nc.vector.tensor_tensor(v32[n % 2][:], BANKS[(5 + n) % 4], bv[:, cs], ALU.add).then_inc(v_ready.sem, 1)

                def queries(q):
                    q_hi.wait(dve, b, q + 1)
                    for a in range(2):
                        p2 = 2 * q + a
                        last = nc.vector.scalar_tensor_tensor(QL[par][:, p2, :], BANKS[(9 + q) % 4][:, a * S:(a + 1) * S],
                                                              bqk[:, 0, p2:p2 + 1], QH[par][:, p2, :], ALU.add, ALU.subtract)
                    last.then_inc(q_lo.sem, 1)

                def maxima(k0, k1):
                    def go():
                        for k in range(k0, k1):
                            s_full.wait(dve, b, k + 1)
                            nc.vector.reduce_max(M[:, k % 2, k - k % 2:k - k % 2 + 2], pS[k % 2][:], AX.X).then_inc(s_max.sem, 1)
                    return go

                def negate():
                    neg_steps.begin(b)
                    s_max.wait(dve, b, 16)
                    neg_steps.link(dve, nc.vector.tensor_scalar(nM[:], M[:], -1.0, None, ALU.mult))
                    neg_steps.link(dve, nc.vector.tensor_copy(NM[:, :, 0, :], nM[:]))
                    neg_steps.link(dve, nc.vector.tensor_tensor(nR[:], nM[:], NM[:, :, 0, :], ALU.subtract))
                    neg_steps.link(dve, nc.vector.tensor_copy(NM[:, :, 1, :], nR[:]))
                    nc.vector.tensor_tensor(NM[:, :, 2, :], nR[:], NM[:, :, 1, :], ALU.subtract).then_inc(neg_parts.sem, 1)
                    neg_steps.end()

                return front_order([inputs], keys, values, queries, maxima, [negate], {8: [make_masks, *ahead(b)]})

            def back(b, par):
                def negated():
                    n_full.wait(dve, b, 1)
                    nc.vector.tensor_copy(MT[par][:], pG[:, 0:P].bitcast(BF16)).then_inc(neg_ready.sem, 1)
                def out(p2):
                    pv_out.wait(dve, b, p2 + 1)
                    if p2 == 0:
                        back_steps.begin(b)
                        o_lo.wait(dve, b, 0)
                    else:
                        o_lo.wait(dve, b, p2 - 1)
                    on_ready.wait(dve, b, p2)
                    back_steps.link(dve, nc.vector.reciprocal(R[:], OS[p2 % 2][:, 1, :]))
                    nc.vector.tensor_tensor(ON[:, p2 % 2, :], OS[p2 % 2][:, 0, :], R[:], ALU.mult).then_inc(on_ready.sem, 1)

                def finish():
                    g_full.wait(dve, b, 1)
                    back_steps.link(dve, nc.vector.tensor_tensor(proj[:], pG[:].rearrange("p (t d) -> p t d", t=2),
                                                                 bo[:].unsqueeze(1).broadcast_to([P, 2, D]), ALU.add))
                    xb = X[:, bass.ds(2 * b, 2), :].rearrange("p t d -> p (t d)")
                    nc.vector.scalar_tensor_tensor(xb, proj[:].rearrange("p t d -> p (t d)"), gates[:, 1:2], xb, ALU.mult, ALU.add)\
                        .then_inc(x_done.sem, 1)
                    back_steps.end()
                return spread(18, {0: [negated]}, {PV[p2] + 1: [lambda p2=p2: out(p2)] for p2 in range(PAIRS)}, {17: [finish]})
            normalised(0, True)
            pipeline(dve, front, back)
            x_done.wait(dve, B, 0)


NE, TOPK, F0 = 8, 2, 512
FK = F0 // P
SLOT_TILES = TOPK * TILES + NE


def moe_router(nc, ctx, X, mean, rstd, XT, gwh, gwl, rows_d, L, consts):
    s = Scope(nc, ctx, "mr")
    xn = [s.sb(f"xn{i}", [P, D]) for i in range(2)]
    row = [s.sb(f"row{i}", [P, 2, D], F16) for i in range(2)]
    pX = [s.ps(f"pX{i}", [P, 2, KD, P], F16) for i in range(2)]
    pL = [s.ps(f"pL{i}", [P, NE]) for i in range(2)]
    xn_ready, hi_ready, lo_ready = s.counter("xn_ready", 1), s.counter("hi_ready", 1), s.counter("lo_ready", 1)
    xt_full, xt_ready, l_full, l_out = s.counter("xt_full", 1), s.counter("xt_ready", 1), s.counter("l_full", 1), s.counter("l_out", 1)
    stored = [s.counter(f"stored{i}", 16) for i in range(2)]
    rows = rows_d.rearrange("(t p) d -> t p d", p=P)
    nc.all_engine_barrier()
    with nc.Block() as block:
        @block.sync
        def _(sp):
            with sp.Fori(0, TILES // 2) as i:
                for q in range(2):
                    t = 2 * i + q
                    lo_ready.wait(sp, t, 1)
                    sp.dma_start(rows[bass.ds(t, 1), :, :].rearrange("a p d -> (a p) d"), row[q][:].rearrange("p a d -> p (a d)"))\
                        .then_inc(stored[q].sem, 16)
            for q in range(2):
                stored[q].wait(sp, TILES // 2, 0)

        @block.vector
        def _(dve):
            def normalise(t, q, first=False):
                if not first:
                    lo_ready.wait(dve, t, -1)
                nc.vector.tensor_scalar(xn[q][:], X[:, bass.ds(t, 1), :].rearrange("p a d -> p (a d)"),
                                        mean[:, bass.ds(t, 1)], rstd[:, bass.ds(t, 1)], ALU.subtract, ALU.mult)\
                    .then_inc(xn_ready.sem, 1)

            def low(t, q):
                hi_ready.wait(dve, t, 1)
                nc.vector.tensor_tensor(row[q][:, 1, :], xn[q][:], row[q][:, 0, :], ALU.subtract).then_inc(lo_ready.sem, 1)

            def keep(t, q):
                xt_full.wait(dve, t, 1)
                nc.vector.tensor_copy(XT[:, :, :, bass.ts(t, P)], pX[q][:]).then_inc(xt_ready.sem, 1)

            normalise(0, 0, True)
            normalise(1, 1, True)
            low(0, 0)
            with dve.Fori(0, TILES // 2 - 1) as i:
                for u in (1, 2):
                    t, q = i * 2 + u, u % 2
                    normalise(t + 1, 1 - q)
                    low(t, q)
                    keep(t - 1, 1 - q)
            low(TILES - 1, 1)
            keep(TILES - 2, 0)
            keep(TILES - 1, 1)

        @block.scalar
        def _(act):
            def high(t, q, pair):
                xn_ready.wait(act, t, 1)
                if pair is not None:
                    stored[q].wait(act, pair, 0)
                    xt_full.wait(act, t, -1)
                nc.scalar.activation(row[q][:, 0, :], xn[q][:], ACT.Copy).then_inc(hi_ready.sem, 1)

            def logits(t, q):
                l_full.wait(act, t, 1)
                nc.scalar.activation(L[:, bass.ds(t, 1), :].rearrange("p a e -> p (a e)"), pL[q][:], ACT.Copy).then_inc(l_out.sem, 1)

            high(0, 0, None)
            high(1, 1, None)
            with act.Fori(0, TILES // 2 - 1) as i:
                for q in range(2):
                    high(i * 2 + 2 + q, q, i + 1)
                    logits(i * 2 + q, q)
            logits(TILES - 2, 0)
            logits(TILES - 1, 1)

        @block.tensor
        def _(pe):
            def transposes(t, q, first=False):
                lo_ready.wait(pe, t, 1)
                if not first:
                    xt_ready.wait(pe, t, -1)
                for part in range(2):
                    for kt in range(KD):
                        last = nc.tensor.transpose(pX[q][:, part, kt, :], row[q][:, part, kt * P:(kt + 1) * P], consts[1][:])
                last.then_inc(xt_full.sem, 1)

            def logits(t, q, first=False):
                xt_ready.wait(pe, t, 1)
                if not first:
                    l_out.wait(pe, t, -1)
                three_products(nc, pL[q][:], lambda kt: XT[:, 0, kt, bass.ts(t, P)], lambda kt: XT[:, 1, kt, bass.ts(t, P)],
                               lambda kt: gwh[:, kt, :], lambda kt: gwl[:, kt, :], KD).then_inc(l_full.sem, 1)

            transposes(0, 0, True)
            transposes(1, 1, True)
            logits(0, 0, True)
            transposes(2, 0)
            logits(1, 1, True)
            with pe.Fori(0, TILES // 2 - 2) as i:
                for u in (3, 4):
                    t, q = i * 2 + u, u % 2
                    transposes(t, q)
                    logits(t - 1, 1 - q)
            transposes(TILES - 1, 1)
            logits(TILES - 2, 0)
            logits(TILES - 1, 1)


def moe_route(nc, ctx, L, gb_d, gates, consts, tok, POS, GW, ETAB):
    s = Scope(nc, ctx, "rt")
    TE = [P, TILES, NE]
    gb = s.sb("gb", [P, NE])
    mx, sm = s.sb("mx", [P, TILES]), s.sb("sm", [P, TILES])
    sc, bi, tmp, cand = s.sb("sc", TE), s.sb("bi", TE), s.sb("tmp", TE), s.sb("cand", TE)
    oh = [s.sb(f"oh{k}", TE) for k in range(TOPK)]
    w = s.sb("w", [P, TOPK, TILES])
    picked = s.sb("picked", TE, BF16)
    eidx_i, eidx = s.sb("eidx_i", TE, I32), s.sb("eidx", TE)
    before, ones = s.sb("before", [P, P], BF16), s.sb("ones", [P, P], BF16)
    excl, tot = s.sb("excl", TE), s.sb("tot", TE)
    scan = [s.sb(f"scan{i}", TE) for i in range(2)]
    steps_i, steps = s.sb("steps_i", [P, NE, TILES], I32), s.sb("steps", [P, NE, TILES])
    more = s.sb("more", [P, NE, TILES])
    tiles = s.sb("tiles", [P, NE])
    ends = [s.sb(f"ends{i}", [P, NE]) for i in range(2)]
    start = s.sb("start", [P, NE])
    posf = s.sb("posf", [P, TOPK, TILES])
    sid_i, sid = s.sb("sid_i", [P, SLOT_TILES], I32), s.sb("sid", [P, SLOT_TILES])
    ecmp, ef = s.sb("ecmp", [P, SLOT_TILES, NE]), s.sb("ef", [P, SLOT_TILES])
    tok_i = s.sb("tok_i", [P, TILES], I32)
    pC = s.ps("pC", [P, 512])
    gb_in, iotas, steps_sem, exp_in, exp_out = s.sem("gb_in"), s.sem("iotas"), s.sem("steps_sem"), s.sem("exp_in"), s.sem("exp_out")
    counts_in, counted = s.sem("counts_in"), s.sem("counted")
    with nc.Block() as block:
        @block.sync
        def _(sp):
            sp.dma_start(gb[:], gb_d.partition_broadcast(P)).then_inc(gb_in, 16)

        @block.gpsimd
        def _(pool):
            nc.gpsimd.memset(before[:], 0.0).then_inc(iotas, 1)
            nc.gpsimd.memset(ones[:], 1.0).then_inc(iotas, 1)
            nc.gpsimd.iota(eidx_i[:], pattern=[[0, TILES], [1, NE]], base=0, channel_multiplier=0).then_inc(iotas, 1)
            nc.gpsimd.iota(steps_i[:], pattern=[[0, NE], [P, TILES]], base=0, channel_multiplier=0).then_inc(iotas, 1)
            nc.gpsimd.iota(sid_i[:], pattern=[[1, SLOT_TILES]], base=0, channel_multiplier=0).then_inc(iotas, 1)
            nc.gpsimd.iota(tok_i[:], pattern=[[P, TILES]], base=0, channel_multiplier=1).then_inc(iotas, 1)
            pool.wait_ge(iotas, 6)
            nc.gpsimd.affine_select(out=before[:], in_=before[:], compare_op=ALU.is_ge, fill=1.0, base=0,
                                    pattern=[[-1, P]], channel_multiplier=1).then_inc(iotas, 1)

        @block.scalar
        def _(act):
            act.wait_ge(exp_in, 1)
            nc.scalar.activation(sc[:], tmp[:], ACT.Exp).then_inc(exp_out, 1)

        @block.tensor
        def _(pe):
            pe.wait_ge(counts_in, 1)
            nc.tensor.matmul(pC[:, 0:256], before[:], picked[:].rearrange("p t e -> p (t e)"), start=True, stop=True)
            nc.tensor.matmul(pC[:, 256:512], ones[:], picked[:].rearrange("p t e -> p (t e)"), start=True, stop=True)\
                .then_inc(counted, 1)

        @block.vector
        def _(dve):
            ch = Chain(steps_sem, 0)
            ch.begin(0)

            def link(ins):
                ch.link(dve, ins)

            def over_e(ap):
                return ap.unsqueeze(2).broadcast_to(TE)

            V = nc.vector
            dve.wait_ge(iotas, 7)
            dve.wait_ge(gb_in, 16)
            for dst, src in ((eidx, eidx_i), (steps, steps_i), (sid, sid_i), (tok, tok_i)):
                link(V.tensor_copy(dst[:], src[:]))
            link(V.reduce_max(mx[:], L[:], AX.X))
            V.tensor_tensor(tmp[:], L[:], over_e(mx[:]), ALU.subtract).then_inc(exp_in, 1)
            dve.wait_ge(exp_out, 1)
            link(V.reduce_sum(sm[:], sc[:], AX.X))
            link(V.reciprocal(sm[:], sm[:]))
            link(V.tensor_tensor(sc[:], sc[:], over_e(sm[:]), ALU.mult))
            link(V.tensor_tensor(bi[:], sc[:], gb[:].unsqueeze(1).broadcast_to(TE), ALU.add))
            for k in range(TOPK):
                link(V.reduce_max(mx[:], bi[:], AX.X))
                link(V.tensor_tensor(tmp[:], bi[:], over_e(mx[:]), ALU.is_equal))
                link(V.scalar_tensor_tensor(cand[:].rearrange("p t e -> p (t e)"), eidx[:].rearrange("p t e -> p (t e)"), -float(NE),
                                            tmp[:].rearrange("p t e -> p (t e)"), ALU.add, ALU.mult))
                link(V.tensor_reduce(mx[:], cand[:], AX.X, ALU.min))
                link(V.tensor_scalar(mx[:], mx[:], float(NE), None, ALU.add))
                link(V.tensor_tensor(oh[k][:], eidx[:], over_e(mx[:]), ALU.is_equal))
                link(V.tensor_tensor(tmp[:], oh[k][:], sc[:], ALU.mult))
                link(V.reduce_sum(w[:, k, :], tmp[:], AX.X))
                if k + 1 < TOPK:
                    link(V.scalar_tensor_tensor(bi[:].rearrange("p t e -> p (t e)"), oh[k][:].rearrange("p t e -> p (t e)"), -3.0e38,
                                                bi[:].rearrange("p t e -> p (t e)"), ALU.mult, ALU.add))
            link(V.tensor_scalar(GW[:], w[:], gates[:, 2:3], None, ALU.mult))
            V.tensor_tensor(picked[:], oh[0][:], oh[1][:], ALU.add).then_inc(counts_in, 1)
            dve.wait_ge(counted, 1)
            link(V.tensor_copy(excl[:].rearrange("p t e -> p (t e)"), pC[:, 0:256]))
            link(V.tensor_copy(tot[:].rearrange("p t e -> p (t e)"), pC[:, 256:512]))
            src, n = tot, 0
            for sh in (1, 2, 4, 8, 16):
                dst = scan[n % 2]
                V.tensor_copy(dst[:, 0:sh, :], src[:, 0:sh, :])
                link(V.tensor_tensor(dst[:, sh:, :], src[:, sh:, :], src[:, :TILES - sh, :], ALU.add))
                src, n = dst, n + 1
            incl = src
            link(V.tensor_tensor(more[:], incl[:, TILES - 1, :].unsqueeze(2).broadcast_to([P, NE, TILES]), steps[:], ALU.is_gt))
            link(V.reduce_sum(tiles[:], more[:], AX.X))
            esrc, n = tiles, 0
            for sh in (1, 2, 4):
                dst = ends[n % 2]
                V.tensor_copy(dst[:, 0:sh], esrc[:, 0:sh])
                link(V.tensor_tensor(dst[:, sh:], esrc[:, sh:], esrc[:, :NE - sh], ALU.add))
                esrc, n = dst, n + 1
            link(V.tensor_tensor(start[:], esrc[:], tiles[:], ALU.subtract))
            link(V.tensor_scalar(start[:], start[:], float(P), None, ALU.mult))
            link(V.tensor_tensor(excl[:], excl[:], incl[:], ALU.add))
            link(V.tensor_tensor(excl[:], excl[:], tot[:], ALU.subtract))
            link(V.tensor_tensor(excl[:], excl[:], start[:].unsqueeze(1).broadcast_to(TE), ALU.add))
            for k in range(TOPK):
                link(V.tensor_tensor(tmp[:], oh[k][:], excl[:], ALU.mult))
                link(V.reduce_sum(posf[:, k, :], tmp[:], AX.X))
            V.tensor_copy(POS[:], posf[:])
            link(V.tensor_tensor(ecmp[:], sid[:].unsqueeze(2).broadcast_to([P, SLOT_TILES, NE]),
                                 esrc[:].unsqueeze(1).broadcast_to([P, SLOT_TILES, NE]), ALU.is_ge))
            link(V.reduce_sum(ef[:], ecmp[:], AX.X))
            link(V.tensor_scalar(ef[:], ef[:], float(NE - 1), None, ALU.min))
            link(V.tensor_copy(ETAB[:], ef[0:1, :]))


def slot_table(nc, ctx, slots_d, tok, POS, IDS, ident):
    s = Scope(nc, ctx, "st")
    NB = 4
    zero = s.sb("zero", [SLOT_TILES, P])
    back = s.sb("back", [SLOT_TILES, P])
    idx = [s.sb(f"idx{i}", [P, 1], U32) for i in range(NB)]
    val = [s.sb(f"val{i}", [P, 1]) for i in range(NB)]
    pI = s.ps("pI", [P, SLOT_TILES])
    zero_ready, zeroed, copied, all_scattered = s.sem("zero_ready"), s.sem("zeroed"), s.sem("copied"), s.sem("all_scattered")
    scattered = [s.counter(f"scattered{i}", 16, start=0) for i in range(NB)]
    table_in, ids_full = s.sem("table_in"), s.sem("ids_full")

    def on_sync(sp):
        sp.wait_ge(zero_ready, 1)
        sp.dma_start(slots_d.rearrange("(s p) a -> s (p a)", p=P), zero[:]).then_inc(zeroed, 16)
        sp.wait_ge(all_scattered, 1)
        sp.dma_start(back[:], slots_d.rearrange("(s p) a -> s (p a)", p=P)).then_inc(table_in, 16)

    def on_pool(pool):
        nc.gpsimd.memset(zero[:], 0.0).then_inc(zero_ready, 1)
        pool.wait_ge(zeroed, 16)

        def scatter(i, first):
            for q in range(NB):
                k, half = q % TOPK, q // TOPK
                t = 2 * i + half
                if not first:
                    scattered[q].wait(pool, i, 0)
                nc.gpsimd.tensor_copy(idx[q][:], POS[:, k, bass.ds(t, 1)]).then_inc(copied, 1)
                nc.gpsimd.tensor_copy(val[q][:], tok[:, bass.ds(t, 1)]).then_inc(copied, 1)
            pool.wait_ge(copied, (i + 1) * 2 * NB)
            nc.gpsimd.nop(nofuse=True)
            for q in range(NB):
                nc.gpsimd.indirect_dma_start(out=slots_d, out_offset=bass.IndirectOffsetOnAxis(ap=idx[q][:], axis=0),
                                             in_=val[q][:], in_offset=None).then_inc(scattered[q].sem, 16)

        scatter(0, True)
        with pool.Fori(1, TILES * TOPK // NB) as i:
            scatter(i, False)
        for q in range(NB):
            scattered[q].wait(pool, TILES * TOPK // NB, 0)
        pool.sem_inc(all_scattered, 1)

    def on_pe(pe):
        pe.wait_ge(table_in, 16)
        nc.tensor.transpose(pI[:], back[:], ident[0:SLOT_TILES, 0:SLOT_TILES]).then_inc(ids_full, 1)

    def on_dve(dve):
        dve.wait_ge(ids_full, 1)
        nc.vector.tensor_copy(IDS[:], pI[:])
    return on_sync, on_pool, on_pe, on_dve


def steps_of(eng, n, step):
    step(0, 0, lambda d: d // 4, True, False)
    with eng.Fori(0, n // 4 - 1) as i:
        for u in range(1, 5):
            step(i * 4 + u, u % 4, lambda d: i + (u + d) // 4, False, False)
    for st in range(n - 3, n):
        step(st, st % 4, lambda d: (st + d) // 4, False, st == n - 1)


def mlp_phase(nc, ctx, tag, n, X, XT, W1, W3, W2, consts, routed, beside=None):
    ident, ident16, gates = consts[0], consts[1], consts[7]
    s = Scope(nc, ctx, tag)
    SG, h = s.sb("SG", [P, F0]), s.sb("h", [P, F0])
    hh, hl = s.sb("hh", [P, FK, P], F16), s.sb("hl", [P, FK, P], F16)
    pG, pU, pH = s.ps("pG", [P, F0]), s.ps("pU", [P, F0]), s.ps("pH", [P, FK * P])
    pY = s.ps("pY", [P, D])
    gate_full, up_full = s.counter("gate_full", 1), s.counter("up_full", 1)
    silu_ready, h_ready = s.counter("silu_ready", 1), s.counter("h_ready", 1)
    ht_full, hh_ready, hl_ready = s.counter("ht_full", 1), s.counter("hh_ready", 1), s.counter("hl_ready", 1)
    y_full, y_out = s.counter("y_full", 1), s.counter("y_out", 1)
    if routed:
        IDS, ETAB, rows_d, y_d = routed
        idx = [s.sb(f"idx{i}", [P, 1], U32) for i in range(4)]
        xg = [s.sb(f"xg{i}", [P, 2, D], F16) for i in range(4)]
        xt = [s.sb(f"xt{i}", [P, 2, KD, P], F16) for i in range(2)]
        yb = [s.sb(f"yb{i}", [P, D]) for i in range(4)]
        pX = s.ps("pX", [P, 2, KD, P], F16)
        idx_ready = s.counter("idx_ready", 1)
        gathered = [s.counter(f"gathered{i}", 16, start=0) for i in range(4)]
        stored = [s.counter(f"stored{i}", 16) for i in range(4)]
        xt_full, xt_ready = s.counter("xt_full", 1), s.counter("xt_ready", 1)

    with nc.Block() as block:
        if routed:
            @block.gpsimd
            def _(pool):
                def gather(st, q):
                    nc.gpsimd.tensor_copy(idx[q][:], IDS[:, bass.ds(st, 1)]).then_inc(idx_ready.sem, 1)
                    idx_ready.wait(pool, st, 1)
                    nc.gpsimd.nop(nofuse=True)
                    nc.gpsimd.indirect_dma_start(out=xg[q][:].rearrange("p a d -> p (a d)"), out_offset=None, in_=rows_d,
                                                 in_offset=bass.IndirectOffsetOnAxis(ap=idx[q][:], axis=0))\
                        .then_inc(gathered[q].sem, 16)

                for q in range(4):
                    gather(q, q)
                with pool.Fori(1, n // 4) as i:
                    for q in range(4):
                        xt_full.wait(pool, i * 4, q - 3)
                        gather(i * 4 + q, q)

            @block.sync
            def _(sp):
                yv = y_d.rearrange("(s p) d -> s p d", p=P)
                with sp.Fori(0, n // 4) as i:
                    for q in range(4):
                        st = i * 4 + q
                        y_out.wait(sp, st, 1)
                        sp.dma_start(yv[bass.ds(st, 1), :, :].rearrange("a p d -> (a p) d"), yb[q][:]).then_inc(stored[q].sem, 16)
                for q in range(4):
                    stored[q].wait(sp, n // 4, 0)

        if beside:
            @block.sync
            def _(sp):
                beside[0](sp)

            @block.gpsimd
            def _(pool):
                beside[1](pool)

        @block.tensor
        def _(pe):
            def xt_transposes(st, q, it):
                gathered[q].wait(pe, it, 16)
                xt_ready.wait(pe, st, 0)
                for part in range(2):
                    for kt in range(KD):
                        last = nc.tensor.transpose(pX[:, part, kt, :], xg[q][:, part, kt * P:(kt + 1) * P], ident16[:])
                last.then_inc(xt_full.sem, 1)

            def expert(st):
                if not routed:
                    return bass.ds(NE, 1)
                return bass.ds(pe.value_load(ETAB[0:1, bass.ds(st, 1)], min_val=0, max_val=NE - 1), 1)

            def down(st):
                e = expert(st)
                hl_ready.wait(pe, st, 1)
                y_out.wait(pe, st, 0)
                three_products(nc, pY[:], lambda k: hh[:, k, :], lambda k: hl[:, k, :],
                               lambda k: W2[0][:, e, k, :].rearrange("p a n -> p (a n)"),
                               lambda k: W2[1][:, e, k, :].rearrange("p a n -> p (a n)"), FK).then_inc(y_full.sem, 1)

            def step(st, q, turn, first, last_one):
                if routed:
                    if first:
                        xt_transposes(0, 0, 0)
                    if not last_one:
                        xt_transposes(st + 1, (q + 1) % 4, turn(1))
                    xt_ready.wait(pe, st, 1)
                    src = xt[q % 2]
                    ah, al = (lambda kt: src[:, 0, kt, :]), (lambda kt: src[:, 1, kt, :])
                else:
                    ah, al = (lambda kt: XT[:, 0, kt, bass.ts(st, P)]), (lambda kt: XT[:, 1, kt, bass.ts(st, P)])
                e = expert(st)
                for out, W, full, free in ((pG, W1, gate_full, silu_ready), (pU, W3, up_full, h_ready)):
                    free.wait(pe, st, 0)
                    three_products(nc, out[:], ah, al, lambda kt: W[0][:, e, kt, :].rearrange("p a n -> p (a n)"),
                                   lambda kt: W[1][:, e, kt, :].rearrange("p a n -> p (a n)"), KD).then_inc(full.sem, 1)
                if not first:
                    down(st - 1)
                h_ready.wait(pe, st, 1)
                hl_ready.wait(pe, st, 0)
                for k in range(FK):
                    last = nc.tensor.transpose(pH[:, k * P:(k + 1) * P], h[:, k * P:(k + 1) * P], ident[:])
                last.then_inc(ht_full.sem, 1)
                if last_one:
                    down(st)
            steps_of(pe, n, step)
            if beside:
                beside[2](pe)

        @block.scalar
        def _(act):
            def step(st, q, turn, first, last_one):
                gate_full.wait(act, st, 1)
                h_ready.wait(act, st, 0)
                nc.scalar.activation(SG[:], pG[:], ACT.Silu).then_inc(silu_ready.sem, 1)
                ht_full.wait(act, st, 1)
                nc.scalar.activation(hh[:].rearrange("p k t -> p (k t)"), pH[:], ACT.Copy).then_inc(hh_ready.sem, 1)
            steps_of(act, n, step)

        @block.vector
        def _(dve):
            def xt_copy(st, q):
                xt_full.wait(dve, st, 1)
                nc.vector.tensor_copy(xt[q % 2][:], pX[:]).then_inc(xt_ready.sem, 1)

            def result(st, q, it):
                y_full.wait(dve, st, 1)
                if routed:
                    stored[q].wait(dve, it, 0)
                    nc.vector.tensor_copy(yb[q][:], pY[:]).then_inc(y_out.sem, 1)
                else:
                    x = X[:, bass.ds(st, 1), :].rearrange("p a d -> p (a d)")
                    nc.vector.scalar_tensor_tensor(x, pY[:], gates[:, 2:3], x, ALU.mult, ALU.add).then_inc(y_out.sem, 1)

            def step(st, q, turn, first, last_one):
                if routed:
                    if first:
                        xt_copy(0, 0)
                    if not last_one:
                        up_full.wait(dve, st, 0)
                        xt_copy(st + 1, q + 1)
                up_full.wait(dve, st, 1)
                silu_ready.wait(dve, st, 1)
                ht_full.wait(dve, st, 0)
                nc.vector.tensor_tensor(h[:], SG[:], pU[:], ALU.mult).then_inc(h_ready.sem, 1)
                if not first:
                    result(st - 1, (q - 1) % 4, turn(-1))
                hh_ready.wait(dve, st, 1)
                nc.vector.tensor_tensor(hl[:].rearrange("p k t -> p (k t)"), pH[:], hh[:].rearrange("p k t -> p (k t)"),
                                        ALU.subtract).then_inc(hl_ready.sem, 1)
                if last_one:
                    result(st, q, turn(0))
            steps_of(dve, n, step)
            if beside:
                beside[3](dve)
            y_out.wait(dve, n, 0)


def moe_combine(nc, ctx, X, st, POS, GW, y_d):
    s = Scope(nc, ctx, "mc")
    NB = 8
    ROUNDS = TILES * TOPK // NB
    idx = [[s.sb(f"idx{u}{i}", [P, 1], U32) for i in range(NB)] for u in range(2)]
    y = [[s.sb(f"y{u}{i}", [P, D]) for i in range(NB)] for u in range(2)]
    idx_ready = s.sem("idx_ready")
    gathered = [[s.counter(f"gathered{u}{i}", 16, start=0) for i in range(NB)] for u in range(2)]
    added = s.counter("added", NB)

    def on_pool(pool):
        def gathers(i, u, first):
            if not first:
                added.wait(pool, i, -NB)
            for q in range(NB):
                nc.gpsimd.tensor_copy(idx[u][q][:], POS[:, q % TOPK, bass.ds(i * (NB // TOPK) + q // TOPK, 1)]).then_inc(idx_ready, 1)
            pool.wait_ge(idx_ready, (i + 1) * NB)
            nc.gpsimd.nop(nofuse=True)
            for q in range(NB):
                nc.gpsimd.indirect_dma_start(out=y[u][q][:], out_offset=None, in_=y_d,
                                             in_offset=bass.IndirectOffsetOnAxis(ap=idx[u][q][:], axis=0)).then_inc(gathered[u][q].sem, 16)

        gathers(0, 0, True)
        gathers(1, 1, True)
        with pool.Fori(1, ROUNDS // 2) as j:
            for u in range(2):
                gathers(j * 2 + u, u, False)

    def on_dve(dve, part, parts):
        with dve.Fori(ROUNDS // 2 * part // parts, ROUNDS // 2 * (part + 1) // parts) as j:
            for u in range(2):
                i = j * 2 + u
                for q in range(NB):
                    t = i * (NB // TOPK) + q // TOPK
                    x = X[:, bass.ds(t, 1), :].rearrange("p a d -> p (a d)")
                    gathered[u][q].wait(dve, j, 16)
                    added.wait(dve, i, q)
                    nc.vector.scalar_tensor_tensor(x, y[u][q][:], GW[:, q % TOPK, bass.ds(t, 1)], x, ALU.mult, ALU.add).then_inc(added.sem, 1)
                    if q % TOPK == TOPK - 1:
                        added.wait(dve, i, q + 1)
                        tile_stats(nc, X, st, t)
    return on_pool, on_dve


def moe(nc, ctx, X, mean, rstd, w_d, gw_d, gb_d, consts, scratch, POS, GW):
    rows_d, slots_d, y_d = scratch
    s = Scope(nc, ctx, "mo")
    W = {n: tuple(s.sb(f"{n}{part}", [P, NE + 1, FK if n == "w2" else KD, D if n == "w2" else F0], F16) for part in "hl")
         for n in ("w1", "w3", "w2")}
    gw = [s.sb(f"gw{part}", [P, KD, NE], F16) for part in "hl"]
    XT = s.sb("XT", [P, 2, KD, TILES * P], F16)
    L = s.sb("L", [P, TILES, NE])
    tok = s.sb("tok", [P, TILES])
    ETAB = s.sb("ETAB", [1, SLOT_TILES], I32)
    IDS = s.sb("IDS", [P, SLOT_TILES], U32)
    flat = "p k n -> p (k n)"
    with ExitStack() as c2:
        load_split(nc, c2, "wg", [(gw_d.rearrange("(k p) n -> p k n", p=P), gw[0][:].rearrange(flat), gw[1][:].rearrange(flat))], KD * NE)
    with ExitStack() as c2:
        jobs = [(w_d[n][e].rearrange("(k p) n -> p k n", p=P), W[n][0][:, e, :, :].rearrange(flat), W[n][1][:, e, :, :].rearrange(flat))
                for n in ("w1", "w3", "w2") for e in range(NE + 1)]
        load_split(nc, c2, "we", jobs, KD * F0)
    with ExitStack() as c2:
        moe_router(nc, c2, X, mean, rstd, XT, gw[0], gw[1], rows_d, L, consts)
    with ExitStack() as c2:
        moe_route(nc, c2, L, gb_d, consts[7], consts, tok, POS, GW, ETAB)
    with ExitStack() as c2:
        table = slot_table(nc, c2, slots_d, tok, POS, IDS, consts[0])
        mlp_phase(nc, c2, "ms", TILES, X, XT, W["w1"], W["w3"], W["w2"], consts, None, table)
    with ExitStack() as c2:
        mlp_phase(nc, c2, "me", SLOT_TILES, X, XT, W["w1"], W["w3"], W["w2"], consts, (IDS, ETAB, rows_d, y_d))


I1 = 704
IT = -(-I1 // P)
LASTROWS = I1 - (IT - 1) * P
BLK = 512
QMAX = 127.0


def quant_weights(nc, ctx, wg_d, wu_d, wd_d, WG, WU, WD, sg, su, WDS, consts):
    ident, identb = consts[0], consts[2]
    s = Scope(nc, ctx, "qw")
    nat = [s.sb(f"nat{i}", [P, IT, D]) for i in range(2)]
    natd = s.sb("natd", [P, KD, I1])
    q = [s.sb(f"q{i}", [P, IT, D], BF16) for i in range(2)]
    qd = s.sb("qd", [P, KD, I1], BF16)
    mx = [s.sb(f"mx{i}", [P, IT]) for i in range(2)]
    rv = [s.sb(f"rv{i}", [P, IT]) for i in range(2)]
    mxd, rvd = s.sb("mxd", [P, KD]), s.sb("rvd", [P, KD])
    diag = s.sb("diag", [P, KD, P])
    ones = s.sb("ones", [P, P])
    pW = [s.ps(f"pW{i}", [P, KD, 4 * P], BF16) for i in range(2)]
    pD = s.ps("pD", [P, KD * P])
    loaded, padded, steps, ready, full, out = (s.sem(x) for x in ("loaded", "padded", "steps", "ready", "full", "out"))
    with nc.Block() as block:
        @block.sync
        def _(sp):
            for n, src in ((0, wg_d), (1, wu_d)):
                sp.dma_start(nat[n][:, 0:IT - 1, :], src[0:(IT - 1) * P, :].rearrange("(m p) d -> p m d", p=P)).then_inc(loaded, 16)
                sp.wait_ge(padded, n + 1)
                sp.dma_start(nat[n][0:LASTROWS, IT - 1, :], src[(IT - 1) * P:I1, :]).then_inc(loaded, 16)
            sp.dma_start(natd[:], wd_d.rearrange("(k p) i -> p k i", p=P)).then_inc(loaded, 16)

        @block.gpsimd
        def _(pool):
            for n in range(2):
                nc.gpsimd.memset(nat[n][:, IT - 1, :], 1.0).then_inc(padded, 1)
            nc.gpsimd.memset(ones[:], 1.0).then_inc(padded, 1)

        @block.vector
        def _(dve):
            ch = Chain(steps, 0)
            ch.begin(0)
            V = nc.vector
            dve.wait_ge(loaded, 80)
            for src, m, r, sc, dst, cols in ((nat[0], mx[0], rv[0], sg, q[0], IT), (nat[1], mx[1], rv[1], su, q[1], IT),
                                             (natd, mxd, rvd, mxd, qd, KD)):
                ch.link(dve, V.tensor_reduce(m[:], src[:], AX.X, ALU.max, apply_absolute_value=True))
                ch.link(dve, V.tensor_scalar(sc[:], m[:], 1.0 / QMAX, None, ALU.mult))
                ch.link(dve, V.reciprocal(r[:], sc[:]))
                for i in range(cols):
                    ch.link(dve, V.tensor_scalar(src[:, i, :], src[:, i, :], r[:, i:i + 1], QMAX, ALU.mult, ALU.min))
                ch.link(dve, V.tensor_scalar(src[:], src[:], -QMAX - 1.0, ROUND, ALU.max, ALU.add))
                V.tensor_scalar(dst[:], src[:], ROUND, None, ALU.subtract).then_inc(ready, 1)
            dve.wait_ge(padded, 3)
            for k in range(KD):
                last = V.tensor_scalar(diag[:, k, :], ident[:], mxd[:, k:k + 1], None, ALU.mult)
            last.then_inc(ready, 1)

        @block.tensor
        def _(pe):
            n = 0
            for w in range(2):
                pe.wait_ge(ready, w + 1)
                for m0 in (0, 4):
                    pe.wait_ge(out, max(n - 1, 0))
                    for m in range(m0, min(m0 + 4, IT)):
                        for k in range(KD):
                            last = nc.tensor.transpose(pW[n % 2][:, k, (m - m0) * P:(m - m0 + 1) * P], q[w][:, m, k * P:(k + 1) * P], identb[:])
                    last.then_inc(full, 1)
                    n += 1
            pe.wait_ge(ready, 3)
            for m0 in (0, 3):
                pe.wait_ge(out, n - 1)
                for m in range(m0, m0 + 3):
                    rows = min(P, I1 - m * P)
                    for k in range(KD):
                        last = nc.tensor.transpose(pW[n % 2][0:rows, k, (m - m0) * P:(m - m0 + 1) * P], qd[:, k, m * P:m * P + rows], identb[:])
                last.then_inc(full, 1)
                n += 1
            pe.wait_ge(ready, 4)
            nc.tensor.matmul(pD[:], ones[:], diag[:].rearrange("p k n -> p (k n)"), start=True, stop=True).then_inc(full, 1)

        @block.scalar
        def _(act):
            n = 0
            for W in (WG, WU):
                for m0 in (0, 4):
                    w = min(4, IT - m0)
                    act.wait_ge(full, n + 1)
                    nc.scalar.activation(W[:, :, m0 * P:(m0 + w) * P], pW[n % 2][:, :, 0:w * P], ACT.Copy).then_inc(out, 1)
                    n += 1
            for m0 in (0, 3):
                act.wait_ge(full, n + 1)
                for m in range(m0, m0 + 3):
                    rows = min(P, I1 - m * P)
                    last = nc.scalar.activation(WD[0:rows, m, :].rearrange("p (k n) -> p k n", k=KD),
                                                pW[n % 2][0:rows, :, (m - m0) * P:(m - m0 + 1) * P], ACT.Copy)
                last.then_inc(out, 1)
                n += 1
            act.wait_ge(full, n + 1)
            nc.scalar.activation(WDS[:], pD[:], ACT.Copy)


def ffn1(nc, ctx, X, mean, rstd, w_d, clip_d, out_d, consts):
    ident, ident16, identb, gates = consts[0], consts[1], consts[2], consts[7]
    s = Scope(nc, ctx, "f1")
    WG, WU = s.sb("WG", [P, KD, IT * P], BF16), s.sb("WU", [P, KD, IT * P], BF16)
    WD = s.sb("WD", [P, IT, D], BF16)
    sg, su = s.sb("sg", [P, IT]), s.sb("su", [P, IT])
    WDS = s.sb("WDS", [P, D])
    with ExitStack() as c2:
        quant_weights(nc, c2, w_d["g"], w_d["u"], w_d["d"], WG, WU, WD, sg, su, WDS, consts)
    NBLK = B * S // BLK
    TB = BLK // P
    XQT = s.sb("XQT", [P, KD, B * S], BF16)
    clip = s.sb("clip", [P, 2])
    sig = s.sb("sig", [P, 2])
    scale, inv = s.sb("scale", [P, 2]), s.sb("inv", [P, 2])
    ones = s.sb("ones", [1, P])
    rounder = s.sb("rounder", [P, 1])

    def scale_steps(name, which, col):
        row, top = s.sb(f"{name}row", [1, P]), s.sb(f"{name}top", [1, 1])
        pR, pB = s.ps(f"{name}pR", [1, P]), s.ps(f"{name}pB", [P, 1])
        col_ready, row_full, top_ready, all_full, st = (s.sem(f"{name}{x}") for x in ("col", "rowf", "topr", "allf", "st"))

        def on_pe(pe):
            pe.wait_ge(col_ready, 1)
            nc.tensor.transpose(pR[:], col, ident[:]).then_inc(row_full, 1)
            pe.wait_ge(top_ready, 1)
            nc.tensor.matmul(pB[:], ones[:], top[:], start=True, stop=True).then_inc(all_full, 1)

        def on_dve(dve, scale_done):
            ch = Chain(st, 0)
            ch.begin(0)
            dve.wait_ge(row_full, 1)
            nc.vector.reduce_max(top[:], pR[:], AX.X).then_inc(top_ready, 1)
            dve.wait_ge(all_full, 1)
            ch.link(dve, nc.vector.tensor_tensor(scale[:, which:which + 1], pB[:], sig[:, which:which + 1], ALU.mult))
            ch.link(dve, nc.vector.tensor_scalar(scale[:, which:which + 1], scale[:, which:which + 1], 1.0 / QMAX, None, ALU.mult))
            nc.vector.reciprocal(inv[:, which:which + 1], scale[:, which:which + 1]).then_inc(scale_done, 1)
        return col_ready, on_pe, on_dve

    with ExitStack() as c2:
        s2 = Scope(nc, c2, "f2")
        XN = s2.sb("XN", [P, TILES, D])
        mx, mcol = s2.sb("mx", [P, TILES]), s2.sb("mcol", [P, 1])
        Q = [s2.sb(f"Q{i}", [P, TB, D], BF16) for i in range(2)]
        pX = [s2.ps(f"pX{i}", [P, KD, BLK], BF16) for i in range(2)]
        clip_in, xn_done, m_done, sig_in, sig_out, sig_done = (s2.sem(x) for x in ("clip_in", "xn_done", "m_done", "sig_in", "sig_out", "sig_done"))
        scale_done, ones_ready, rounded, capped = s2.sem("scale_done"), s2.sem("ones_ready"), s2.counter("rounded", 1), s2.counter("capped", 1)
        q_ready, xt_full, xt_out = s2.counter("q_ready", 1), s2.counter("xt_full", 1), s2.counter("xt_out", 1)
        keep = s.ctx
        s.ctx = c2
        col_ready, scale_pe, scale_dve = scale_steps("a", 0, mcol[:])
        s.ctx = keep
        nc.all_engine_barrier()
        with nc.Block() as block:
            @block.sync
            def _(sp):
                sp.dma_start(clip[:, 0:1], clip_d[0].partition_broadcast(P)).then_inc(clip_in, 16)
                sp.dma_start(clip[:, 1:2], clip_d[1].partition_broadcast(P)).then_inc(clip_in, 16)

            @block.gpsimd
            def _(pool):
                nc.gpsimd.memset(rounder[:], ROUND).then_inc(ones_ready, 1)
                nc.gpsimd.memset(ones[:], 1.0).then_inc(ones_ready, 1)

            @block.scalar
            def _(act):
                act.wait_ge(clip_in, 32)
                nc.scalar.activation(sig[:], clip[:], ACT.Exp, scale=-1.0).then_inc(sig_out, 1)
                act.wait_ge(scale_done, 1)
                act.wait_ge(ones_ready, 2)

                def round_block(n):
                    xv = XN[:, bass.ts(n, TB), :].rearrange("p t d -> p (t d)")
                    nc.scalar.activation(xv, xv, ACT.Identity, bias=rounder[:], scale=inv[:, 0:1]).then_inc(rounded.sem, 1)

                def keep(n, q):
                    xt_full.wait(act, n, 1)
                    nc.scalar.activation(XQT[:, :, bass.ts(n, BLK)], pX[q][:], ACT.Copy).then_inc(xt_out.sem, 1)
                round_block(0)
                with act.Fori(0, NBLK // 2 - 1) as i:
                    for q in range(2):
                        round_block(i * 2 + q + 1)
                        keep(i * 2 + q, q)
                round_block(NBLK - 1)
                keep(NBLK - 2, 0)
                keep(NBLK - 1, 1)

            @block.vector
            def _(dve):
                V = nc.vector
                with dve.Fori(0, TILES // 4) as i:
                    for u in range(4):
                        t = i * 4 + u
                        last = V.tensor_scalar(XN[:, bass.ds(t, 1), :].rearrange("p a d -> p (a d)"), X[:, bass.ds(t, 1), :].rearrange("p a d -> p (a d)"),
                                               mean[:, bass.ds(t, 1)], rstd[:, bass.ds(t, 1)], ALU.subtract, ALU.mult)
                    last.then_inc(xn_done, 1)
                dve.wait_ge(xn_done, TILES // 4)
                V.tensor_reduce(mcol[:], XN[:].rearrange("p t d -> p (t d)"), AX.X, ALU.max, apply_absolute_value=True).then_inc(col_ready, 1)
                dve.wait_ge(sig_out, 1)
                V.tensor_scalar(sig[:], sig[:], 1.0, None, ALU.add).then_inc(sig_done, 1)
                dve.wait_ge(sig_done, 1)
                V.reciprocal(sig[:], sig[:]).then_inc(sig_done, 1)
                dve.wait_ge(sig_done, 2)
                scale_dve(dve, scale_done)
                dve.wait_ge(scale_done, 1)
                with dve.Fori(0, NBLK // 2) as i:
                    for q in range(2):
                        n = i * 2 + q
                        rounded.wait(dve, n, 1)
                        xt_full.wait(dve, i * 2, 0)
                        qv = Q[q][:].rearrange("p t d -> p (t d)")
                        V.tensor_scalar(qv, XN[:, bass.ts(n, TB), :].rearrange("p t d -> p (t d)"), ROUND, QMAX, ALU.subtract, ALU.min)\
                            .then_inc(capped.sem, 1)
                        capped.wait(dve, n, 1)
                        V.tensor_scalar(qv, qv, -QMAX - 1.0, None, ALU.max).then_inc(q_ready.sem, 1)

            @block.tensor
            def _(pe):
                pe.wait_ge(ones_ready, 2)
                scale_pe(pe)
                with pe.Fori(0, NBLK // 2) as i:
                    for q in range(2):
                        n = i * 2 + q
                        q_ready.wait(pe, n, 1)
                        xt_out.wait(pe, i * 2, 0)
                        for t in range(TB):
                            for k in range(KD):
                                last = nc.tensor.transpose(pX[q][:, k, t * P:(t + 1) * P], Q[q][:, t, k * P:(k + 1) * P], identb[:])
                        last.then_inc(xt_full.sem, 1)

    HT = s.sb("HT", [P, NBLK, IT, BLK])
    hmx, hcol = s.sb("hmx", [P, NBLK, IT]), s.sb("hcol", [P, 1])
    with ExitStack() as c2:
        s2 = Scope(nc, c2, "f3")
        SG = [s2.sb(f"SG{i}", [P, BLK]) for i in range(2)]
        sgx, sux = s2.sb("sgx", [P, IT]), s2.sb("sux", [P, IT])
        pG = [s2.ps(f"pG{i}", [P, BLK]) for i in range(2)]
        pU = [s2.ps(f"pU{i}", [P, BLK]) for i in range(2)]
        scales, cleared = s2.sem("scales"), s2.sem("cleared")
        g_full, u_full = s2.counter("g_full", IT), s2.counter("u_full", IT)
        silu, h_ready, maxed = s2.counter("silu", IT), s2.counter("h_ready", IT), s2.counter("maxed", IT)
        with nc.Block() as block:
            @block.gpsimd
            def _(pool):
                nc.gpsimd.memset(HT[64:P, :, IT - 1, :], 0.0).then_inc(cleared, 1)

            @block.tensor
            def _(pe):
                with pe.Fori(0, NBLK) as n:
                    for m in range(IT):
                        for bank, W, full, free in ((pG, WG, g_full, silu), (pU, WU, u_full, h_ready)):
                            free.wait(pe, n, max(m - 1, 0))
                            for k in range(KD):
                                last = nc.tensor.matmul(bank[m % 2][:], W[:, k, m * P:(m + 1) * P], XQT[:, k, bass.ts(n, BLK)],
                                                        start=(k == 0), stop=(k == KD - 1))
                            last.then_inc(full.sem, 1)

            @block.scalar
            def _(act):
                act.wait_ge(scales, 2)
                with act.Fori(0, NBLK) as n:
                    for m in range(IT):
                        rows = min(P, I1 - m * P)
                        g_full.wait(act, n, m + 1)
                        h_ready.wait(act, n, max(m - 1, 0))
                        nc.scalar.activation(SG[m % 2][0:rows, :], pG[m % 2][0:rows, :], ACT.Silu, scale=sgx[0:rows, m:m + 1]).then_inc(silu.sem, 1)

            @block.vector
            def _(dve):
                V = nc.vector
                V.tensor_scalar(sgx[:], sg[:], scale[:, 0:1], None, ALU.mult).then_inc(scales, 1)
                V.tensor_scalar(sux[:], su[:], scale[:, 0:1], None, ALU.mult).then_inc(scales, 1)
                dve.wait_ge(scales, 2)
                dve.wait_ge(cleared, 1)

                def largest(n, m):
                    h_ready.wait(dve, n, m + 1)
                    V.tensor_reduce(hmx[:, bass.ds(n, 1), m], HT[:, bass.ds(n, 1), m, :].rearrange("p a t -> p (a t)"), AX.X, ALU.max,
                                    apply_absolute_value=True).then_inc(maxed.sem, 1)

                with dve.Fori(0, NBLK) as n:
                    for m in range(IT):
                        rows = min(P, I1 - m * P)
                        u_full.wait(dve, n, m + 1)
                        silu.wait(dve, n, m + 1)
                        V.scalar_tensor_tensor(HT[0:rows, bass.ds(n, 1), m, :].rearrange("p a t -> p (a t)"), pU[m % 2][0:rows, :],
                                               sux[0:rows, m:m + 1], SG[m % 2][0:rows, :], ALU.mult, ALU.mult).then_inc(h_ready.sem, 1)
                        if m:
                            largest(n, m - 1)
                    largest(n, IT - 1)
                maxed.wait(dve, NBLK, 0)
                V.tensor_reduce(hcol[:], hmx[:].rearrange("p n m -> p (n m)"), AX.X, ALU.max)

    with ExitStack() as c2:
        s2 = Scope(nc, c2, "f4")
        row_scale = s2.sb("row_scale", [P, D])
        HQ = [s2.sb(f"HQ{i}", [P, IT, BLK], BF16) for i in range(2)]
        y = [s2.sb(f"y{i}", [P, 2, D]) for i in range(2)]
        pY = [s2.ps(f"pY{i}", [P, 2, D]) for i in range(2)]
        scale_done, row_ready, rounded, capped = s2.sem("scale_done"), s2.sem("row_ready"), s2.counter("rounded", 1), s2.counter("capped", 1)
        hq_ready, y_full, scaled, added = s2.counter("hq_ready", 1), s2.counter("y_full", 2), s2.counter("scaled", 2), s2.counter("added", 2)
        stored = s2.sem("stored")
        keep = s.ctx
        s.ctx = c2
        col_ready, scale_pe, scale_dve = scale_steps("b", 1, hcol[:])
        s.ctx = keep
        nc.all_engine_barrier()
        with nc.Block() as block:
            @block.vector
            def _(dve):
                V = nc.vector
                dve.sem_inc(col_ready, 1)
                scale_dve(dve, scale_done)
                dve.wait_ge(scale_done, 1)
                V.tensor_scalar(row_scale[:], WDS[:], scale[:, 1:2], gates[:, 3:4], ALU.mult, ALU.mult).then_inc(row_ready, 1)
                dve.wait_ge(row_ready, 1)

                def round_block(n, q):
                    hq = HQ[q][:].rearrange("p m t -> p (m t)")
                    rounded.wait(dve, n, 1)
                    if not isinstance(n, int):
                        y_full.wait(dve, n, -2)
                    V.tensor_scalar(hq, HT[:, bass.ds(n, 1), :, :].rearrange("p a m t -> p (a m t)"), ROUND, QMAX, ALU.subtract, ALU.min)\
                        .then_inc(capped.sem, 1)
                    capped.wait(dve, n, 1)
                    V.tensor_scalar(hq, hq, -QMAX - 1.0, None, ALU.max).then_inc(hq_ready.sem, 1)

                def results(n, first=False):
                    for half in range(2):
                        y_full.wait(dve, n, half + 1)
                        if not first:
                            added.wait(dve, n, half - 1)
                        V.tensor_tensor(y[half][:], pY[half][:], row_scale[:].unsqueeze(1).broadcast_to([P, 2, D]), ALU.mult)\
                            .then_inc(scaled.sem, 1)

                round_block(0, 0)
                round_block(1, 1)
                results(0, True)
                with dve.Fori(0, NBLK // 2 - 1) as i:
                    for q in range(2):
                        round_block(i * 2 + 2 + q, q)
                        results(i * 2 + 1 + q)
                results(NBLK - 1)

            @block.gpsimd
            def _(pool):
                with pool.Fori(0, NBLK) as n:
                    for half in range(2):
                        scaled.wait(pool, n, half + 1)
                        x = X[:, bass.ds(n * 4 + 2 * half, 2), :].rearrange("p t d -> p (t d)")
                        nc.gpsimd.tensor_tensor(x, x, y[half][:].rearrange("p t d -> p (t d)"), ALU.add).then_inc(added.sem, 1)

            @block.scalar
            def _(act):
                act.wait_ge(scale_done, 1)
                with act.Fori(0, NBLK) as n:
                    hv = HT[:, bass.ds(n, 1), :, :].rearrange("p a m t -> p (a m t)")
                    nc.scalar.activation(hv, hv, ACT.Identity, bias=rounder[:], scale=inv[:, 1:2]).then_inc(rounded.sem, 1)

            @block.tensor
            def _(pe):
                scale_pe(pe)
                with pe.Fori(0, NBLK // 2) as i:
                    for q in range(2):
                        n = i * 2 + q
                        hq_ready.wait(pe, n, 1)
                        for half in range(2):
                            scaled.wait(pe, n, 0)
                            for j in range(2):
                                t = 2 * half + j
                                for m in range(IT):
                                    rows = min(P, I1 - m * P)
                                    last = nc.tensor.matmul(pY[half][:, j, :], HQ[q][0:rows, m, t * P:(t + 1) * P], WD[0:rows, m, :],
                                                            start=(m == 0), stop=(m == IT - 1))
                            last.then_inc(y_full.sem, 1)

            @block.sync
            def _(sp):
                ov = out_d.rearrange("(t p) d -> p t d", p=P)
                with sp.Fori(0, NBLK) as n:
                    added.wait(sp, n, 2)
                    sp.dma_start(ov[:, bass.ds(n * 4, 4), :], X[:, bass.ds(n * 4, 4), :]).then_inc(stored, 16)
                sp.wait_ge(stored, 16 * NBLK)


def network(nc, out_d, scratch, x_d, ctxT_d, itok_d, mask_d, maskT_d, g_x_d, g_f_d, w0, b0, wm, gate_w_d, gate_b_d, w1, b1, wf, clip_d):
    with ExitStack() as ctx:
        s = Scope(nc, ctx, "g")
        X = s.sb("X", [P, TILES, D])
        consts = (s.sb("ident", [P, P]), s.sb("ident16", [P, P], F16), s.sb("identb", [P, P], BF16), s.sb("is0", [P, 1]),
                  s.sb("not0", [P, 1]), s.sb("cosT", [P, TILES, H]), s.sb("sinT", [P, TILES, H]), s.sb("gates", [P, 4]))
        POS, GW = s.sb("POS", [P, TOPK, TILES], U32), s.sb("GW", [P, TOPK, TILES])
        st, mean, rstd = s.sb("st", [P, TILES, 6]), s.sb("mean", [P, TILES]), s.sb("rstd", [P, TILES])
        with ExitStack() as c2:
            setup_phase(nc, c2, X, x_d, itok_d, g_x_d, g_f_d, consts)
        with ExitStack() as c2:
            layernorm_stats(nc, c2, "l0", X, st, mean, rstd, whole=True)
        with ExitStack() as c2:
            attention0(nc, c2, X, mean, rstd, ctxT_d, w0, b0, consts)
        end_of_part(nc)
        with ExitStack() as c2:
            layernorm_stats(nc, c2, "l1", X, st, mean, rstd, whole=True)
        with ExitStack() as c2:
            moe(nc, c2, X, mean, rstd, wm, gate_w_d, gate_b_d, consts, scratch, POS, GW)
        end_of_part(nc)
        with ExitStack() as c2:
            attention1(nc, c2, X, mean, rstd, ctxT_d, mask_d, maskT_d, w1, b1, consts, (st, POS, GW, scratch[2]))
        end_of_part(nc)
        with ExitStack() as c2:
            layernorm_stats(nc, c2, "l3", X, st, mean, rstd, whole=True)
        with ExitStack() as c2:
            ffn1(nc, c2, X, mean, rstd, wf, clip_d, out_d, consts)


def kernel(**inputs):
    import concourse.bacc as bacc
    from concourse.bass_utils import run_bass_kernel_spmd as run

    nc = bacc.Bacc("TRN2", target_bir_lowering=False, num_devices=1)
    arrays = {}

    def given(name, a):
        arrays[name] = np.ascontiguousarray(a)
        return nc.dram_tensor(name, arrays[name].shape, mybir.dt.from_np(arrays[name].dtype), kind="ExternalInput").ap()

    v = {name: np.asarray(a) for name, a in inputs.items()}
    x = given("x", v["x"].reshape(B * S, D))
    ctxT = given("ctxT", v["ctx_1024"].reshape(B * S, D).T)
    itok = given("itok", v["itok_BxSx2_0_63"].reshape(B * S, 2))
    m = v["mask_Bx1xSxS2_ik1"].reshape(B, S, S)
    mask, maskT = given("mask", m.reshape(B * S, S)), given("maskT", m.transpose(0, 2, 1).reshape(B * S, S))
    g_x, g_f = given("g_xattn", v["g_xattn"]), given("g_ffn", v["g_ffn"])
    w0 = {n: given(f"w0{n}", v[f"L0_xattn_W{n}"].T) for n in "qkvp"}
    b0 = {n: given(f"b0{n}", v[f"L0_xattn_b{n}"]) for n in "qkvp"}
    wm = {}
    for n in ("w1", "w3", "w2"):
        routed = given(f"m{n}", v[f"L0_ffn_{n}"].transpose(0, 2, 1))
        shared = given(f"ms{n}", v[f"L0_ffn_s{n}"].T)
        wm[n] = [routed[e, :, :] for e in range(NE)] + [shared]
    gate_w, gate_b = given("gate_w", v["L0_ffn_gate_w"].T), given("gate_bias", v["L0_ffn_gate_bias"])
    w1 = {n: given(f"w1{n}", v[f"L1_xattn_W_{n}"]) for n in "qkvo"}
    b1 = {n: given(f"b1{n}", v[f"L1_xattn_b_{n}"].reshape(H // 2, P).T if n in "qk" else v[f"L1_xattn_b_{n}"]) for n in "qkvo"}
    wf = {n[0]: given(f"wf{n}", v[f"L1_ffn_w_{n}"]) for n in ("gate", "up", "down")}
    clip = (given("clip_x", v["L1_ffn_clip_x"]), given("clip_down", v["L1_ffn_clip_down"]))
    scratch = (nc.dram_tensor("rows", [B * S, 2 * D], F16, kind="Internal").ap(),
               nc.dram_tensor("slots", [SLOT_TILES * P, 1], F32, kind="Internal").ap(),
               nc.dram_tensor("ys", [SLOT_TILES * P, D], F32, kind="Internal").ap())
    out = nc.dram_tensor("out", [B * S, D], F32, kind="ExternalOutput").ap()
    network(nc, out, scratch, x, ctxT, itok, mask, maskT, g_x, g_f, w0, b0, wm, gate_w, gate_b, w1, b1, wf, clip)
    r = run(nc, [arrays], core_ids=[0])
    return r.results[0]["out"].reshape(B, S, D)
```
